# Optimizing a Trainium2 kernel written in Bass

```python
import numpy as np
import jax
import jax.numpy as jnp

def _softmax(x, axis=-1):
    return jax.nn.softmax(x, axis=axis)

def _gelu(x):
    return jax.nn.gelu(x, approximate=True)

def _silu(x):
    return jax.nn.silu(x)

def _sigmoid(x):
    return jax.nn.sigmoid(x)

def _layernorm(x, axis=-1, eps=1e-05):
    m = jnp.mean(x, axis=axis, keepdims=True)
    v = jnp.var(x, axis=axis, keepdims=True)
    return (x - m) / jnp.sqrt(v + eps)

def _scatter_add(tgt, idx, src, axis=0):
    return tgt.at[idx].add(src)

def _segment_sum(src, seg, n):
    return jax.ops.segment_sum(src, seg, n)
kernel_name = 'mk_xattn_seq_d4_seqx_r8_2c6d31'

def setup_inputs(seed: int=0):
    np.random.seed(seed)
    _w = jnp.asarray

    def _rec_inputs():
        import jax
        import jax.numpy as jnp
        _rk = jax.random.key(seed)
        x = 7.22e-05 + 1 * jax.random.normal(jax.random.fold_in(_rk, 1), (8, 256, 128), jnp.float32)
        _lenS = 256 - jax.random.randint(jax.random.fold_in(_rk, 7), (8,), 0, max(1, 256 // 4) + 1, jnp.int32)
        _lenS2 = 256 - jax.random.randint(jax.random.fold_in(_rk, 8), (8,), 0, max(1, 256 // 4) + 1, jnp.int32)
        _ctx_768P = jax.random.normal(jax.random.fold_in(_rk, 11), (8, 16, 96), jnp.float32)
        _ctx_768c = jax.random.dirichlet(jax.random.fold_in(_rk, 511), 0.3 * jnp.ones((16,), jnp.float32), (8, 256))
        _ctx_768t = jnp.einsum('bsk,bkd->bsd', _ctx_768c, _ctx_768P)
        _ctx_768t = _ctx_768t * jax.lax.rsqrt(jnp.mean(jnp.square(_ctx_768t)) + 1e-12) * 0.953939
        ctx_768 = 0.000651243 + 0.998673 * (_ctx_768t + 0.3 * jax.random.normal(jax.random.fold_in(_rk, 611), (8, 256, 96), jnp.float32))
        _validS = jnp.arange(256)[None, :] < _lenS[:, None]
        _validS2 = jnp.arange(256)[None, :] < _lenS2[:, None]
        _causal = jnp.tril(jnp.ones((256, 256), dtype=bool))
        mask_BxS_bf0 = jnp.logical_not(jnp.ones((8, 256), dtype=bool))
        mask_BxS2_bf0 = jnp.logical_not(jnp.ones((8, 256), dtype=bool))
        return (x, ctx_768, mask_BxS_bf0, mask_BxS2_bf0)
    x, ctx_768, mask_BxS_bf0, mask_BxS2_bf0 = _rec_inputs()

    def _L0_xattn_setup():
        import jax, jax.numpy as jnp
        import numpy as np
        HEADS = 16
        D_HEAD = 64
        EPS = 1e-05

        def _ln(x, g, b):
            m = jnp.mean(x, axis=-1, keepdims=True)
            v = jnp.var(x, axis=-1, keepdims=True)
            return (x - m) * jax.lax.rsqrt(v + EPS) * g + b

        def _attn(xq, xc, Wq, Wk, Wv, Wo, bo):
            B, N, _ = xq.shape
            S = xc.shape[1]
            q = (xq @ Wq).reshape(B, N, HEADS, D_HEAD)
            k = (xc @ Wk).reshape(B, S, HEADS, D_HEAD)
            v = (xc @ Wv).reshape(B, S, HEADS, D_HEAD)
            scale = D_HEAD ** (-0.5)
            scores = jnp.einsum('bnhd,bshd->bhns', q, k) * scale
            attn = jax.nn.softmax(scores, axis=-1)
            out = jnp.einsum('bhns,bshd->bnhd', attn, v).reshape(B, N, HEADS * D_HEAD)
            return out @ Wo + bo

        def _geglu_ff(x, Wp, bp, Wf, bf):
            h = x @ Wp + bp
            a, gate = jnp.split(h, 2, axis=-1)
            return a * jax.nn.gelu(gate, approximate=False) @ Wf + bf
        key = jax.random.key(seed)
        ks = jax.random.split(key, 16)
        dim, ctx, inner, ffin = (128, 96, HEADS * D_HEAD, 4 * 128)

        def w(k, i, o):
            return jax.random.normal(k, (i, o), jnp.float32) * i ** (-0.5)
        inp = {'x': jax.random.normal(ks[0], (4, 256, dim), jnp.float32), 'context': jax.random.normal(ks[1], (4, 77, ctx), jnp.float32), 'Wq1': w(ks[2], dim, inner), 'Wk1': w(ks[3], dim, inner), 'Wv1': w(ks[4], dim, inner), 'Wo1': w(ks[5], inner, dim), 'bo1': jnp.zeros((dim,), jnp.float32), 'Wq2': w(ks[6], dim, inner), 'Wk2': w(ks[7], ctx, inner), 'Wv2': w(ks[8], ctx, inner), 'Wo2': w(ks[9], inner, dim), 'bo2': jnp.zeros((dim,), jnp.float32), 'Wp': w(ks[10], dim, 2 * ffin), 'bp': jnp.zeros((2 * ffin,), jnp.float32), 'Wf': w(ks[11], ffin, dim), 'bf': jnp.zeros((dim,), jnp.float32), 'g1': jnp.ones((dim,), jnp.float32), 'b1': jnp.zeros((dim,), jnp.float32), 'g2': jnp.ones((dim,), jnp.float32), 'b2': jnp.zeros((dim,), jnp.float32), 'g3': jnp.ones((dim,), jnp.float32), 'b3': jnp.zeros((dim,), jnp.float32)}
        return inp
    _L0_xattn_all = _L0_xattn_setup()
    _L0_xattn_in = {k: v for k, v in _L0_xattn_all.items() if k in ('Wq1', 'Wk1', 'Wv1', 'Wo1', 'bo1', 'Wq2', 'Wk2', 'Wv2', 'Wo2', 'bo2', 'Wp', 'bp', 'Wf', 'bf', 'g1', 'b1', 'g2', 'b2', 'g3', 'b3')}
    del _L0_xattn_all

    def _L1_xattn_setup():
        import jax, jax.numpy as jnp
        import numpy as np
        D_DEC, D_ENC, H, D_MLP = (128, 96, 16, 512)
        HD = D_DEC // H

        def _layernorm(x, w, b, eps=1e-05):
            m = x.mean(-1, keepdims=True)
            v = ((x - m) ** 2).mean(-1, keepdims=True)
            return (x - m) / jnp.sqrt(v + eps) * w + b

        def _decoder_block(x, enc, tgt_mask, enc_mask, ln1_w, ln1_b, qkv_w, qkv_b, proj_w, proj_b, ln2_w, ln2_b, q_w, q_b, k_w, k_b, v_w, v_b, out_w, out_b, ln3_w, ln3_b, mlp1_w, mlp1_b, mlp2_w, mlp2_b):
            B, T, C = x.shape
            S = enc.shape[1]
            scale = HD ** (-0.5)
            neg = jnp.asarray(-jnp.inf, x.dtype)
            h = _layernorm(x, ln1_w, ln1_b)
            qkv = (h @ qkv_w + qkv_b).reshape(B, T, 3, H, HD)
            q, k, v = [qkv[:, :, i].transpose(0, 2, 1, 3) for i in range(3)]
            attn = jnp.einsum('bhtd,bhsd->bhts', q, k) * scale
            causal = jnp.triu(jnp.ones((T, T), bool), 1)
            attn = jnp.where(causal[None, None], neg, attn)
            attn = jnp.where(tgt_mask[:, None, None, :], neg, attn)
            attn = jax.nn.softmax(attn, axis=-1)
            sa = jnp.einsum('bhts,bhsd->bhtd', attn, v).transpose(0, 2, 1, 3).reshape(B, T, C)
            x = x + sa @ proj_w + proj_b
            h = _layernorm(x, ln2_w, ln2_b)
            q = (h @ q_w + q_b).reshape(B, T, H, HD).transpose(0, 2, 1, 3)
            k = (enc @ k_w + k_b).reshape(B, S, H, HD).transpose(0, 2, 1, 3)
            v = (enc @ v_w + v_b).reshape(B, S, H, HD).transpose(0, 2, 1, 3)
            attn = jnp.einsum('bhtd,bhsd->bhts', q, k) * scale
            attn = jnp.where(enc_mask[:, None, None, :], neg, attn)
            attn = jax.nn.softmax(attn, axis=-1)
            ca = jnp.einsum('bhts,bhsd->bhtd', attn, v).transpose(0, 2, 1, 3).reshape(B, T, C)
            x = x + ca @ out_w + out_b
            h = _layernorm(x, ln3_w, ln3_b)
            h = jax.nn.gelu(h @ mlp1_w + mlp1_b, approximate=False)
            x = x + h @ mlp2_w + mlp2_b
            return x
        key = jax.random.key(seed)
        ks = jax.random.split(key, 16)
        B, T, S = (4, 128, 72)

        def lin(k, din, dout):
            kw, kb = jax.random.split(k)
            bound = 1.0 / np.sqrt(din)
            W = jax.random.uniform(kw, (din, dout), jnp.float32, -bound, bound)
            b = jax.random.uniform(kb, (dout,), jnp.float32, -bound, bound)
            return (W, b)
        qkv_w, qkv_b = lin(ks[0], D_DEC, 3 * D_DEC)
        proj_w, proj_b = lin(ks[1], D_DEC, D_DEC)
        q_w, q_b = lin(ks[2], D_DEC, D_DEC)
        k_w, k_b = lin(ks[3], D_ENC, D_DEC)
        v_w, v_b = lin(ks[4], D_ENC, D_DEC)
        out_w, out_b = lin(ks[5], D_DEC, D_DEC)
        mlp1_w, mlp1_b = lin(ks[6], D_DEC, D_MLP)
        mlp2_w, mlp2_b = lin(ks[7], D_MLP, D_DEC)
        return {'x': jax.random.normal(ks[8], (B, T, D_DEC), jnp.float32), 'enc': jax.random.normal(ks[9], (B, S, D_ENC), jnp.float32), 'tgt_key_padding_mask': jnp.zeros((B, T), bool), 'enc_padding_mask': jnp.zeros((B, S), bool), 'ln1_w': jnp.ones((D_DEC,)), 'ln1_b': jnp.zeros((D_DEC,)), 'qkv_w': qkv_w, 'qkv_b': qkv_b, 'proj_w': proj_w, 'proj_b': proj_b, 'ln2_w': jnp.ones((D_DEC,)), 'ln2_b': jnp.zeros((D_DEC,)), 'q_w': q_w, 'q_b': q_b, 'k_w': k_w, 'k_b': k_b, 'v_w': v_w, 'v_b': v_b, 'out_w': out_w, 'out_b': out_b, 'ln3_w': jnp.ones((D_DEC,)), 'ln3_b': jnp.zeros((D_DEC,)), 'mlp1_w': mlp1_w, 'mlp1_b': mlp1_b, 'mlp2_w': mlp2_w, 'mlp2_b': mlp2_b}
    _L1_xattn_all = _L1_xattn_setup()
    _L1_xattn_in = {k: v for k, v in _L1_xattn_all.items() if k in ('ln1_w', 'ln1_b', 'qkv_w', 'qkv_b', 'proj_w', 'proj_b', 'ln2_w', 'ln2_b', 'q_w', 'q_b', 'k_w', 'k_b', 'v_w', 'v_b', 'out_w', 'out_b', 'ln3_w', 'ln3_b', 'mlp1_w', 'mlp1_b', 'mlp2_w', 'mlp2_b')}
    del _L1_xattn_all

    def _L2_xattn_setup():
        import jax, jax.numpy as jnp
        import numpy as np
        B, S, D = (4, 256, 128)
        CTX_LEN, CTX_DIM = (77, 96)
        H, DH = (16, 64)
        INNER = H * DH
        MULT = 4
        EPS = 1e-05

        def _layernorm(x, g, b):
            mu = jnp.mean(x, axis=-1, keepdims=True)
            var = jnp.var(x, axis=-1, keepdims=True)
            return (x - mu) * jax.lax.rsqrt(var + EPS) * g + b

        def _attn(xq, xkv, wq, wk, wv, wo, bo):
            b, sq, _ = xq.shape
            sk = xkv.shape[1]
            q = (xq @ wq).reshape(b, sq, H, DH)
            k = (xkv @ wk).reshape(b, sk, H, DH)
            v = (xkv @ wv).reshape(b, sk, H, DH)
            score = jnp.einsum('bqhd,bkhd->bhqk', q, k) * DH ** (-0.5)
            w = jax.nn.softmax(score, axis=-1)
            o = jnp.einsum('bhqk,bkhd->bqhd', w, v).reshape(b, sq, INNER)
            return o @ wo + bo

        def _block(x, context, ln1_g, ln1_b, ln2_g, ln2_b, ln3_g, ln3_b, a1_wq, a1_wk, a1_wv, a1_wo, a1_bo, a2_wq, a2_wk, a2_wv, a2_wo, a2_bo, ff_w1, ff_b1, ff_w2, ff_b2):
            x = _attn(_layernorm(x, ln1_g, ln1_b), _layernorm(x, ln1_g, ln1_b), a1_wq, a1_wk, a1_wv, a1_wo, a1_bo) + x
            x = _attn(_layernorm(x, ln2_g, ln2_b), context, a2_wq, a2_wk, a2_wv, a2_wo, a2_bo) + x
            h = _layernorm(x, ln3_g, ln3_b) @ ff_w1 + ff_b1
            u, gate = jnp.split(h, 2, axis=-1)
            x = u * jax.nn.gelu(gate, approximate=False) @ ff_w2 + ff_b2 + x
            return x
        key = jax.random.key(seed)
        ks = jax.random.split(key, 14)
        nrm = lambda k, shape: jax.random.normal(k, shape, dtype=jnp.float32) * 0.02
        return {'x': jax.random.normal(ks[0], (B, S, D), dtype=jnp.float32), 'context': jax.random.normal(ks[1], (B, CTX_LEN, CTX_DIM), dtype=jnp.float32), 'ln1_g': jnp.ones((D,), jnp.float32), 'ln1_b': jnp.zeros((D,), jnp.float32), 'ln2_g': jnp.ones((D,), jnp.float32), 'ln2_b': jnp.zeros((D,), jnp.float32), 'ln3_g': jnp.ones((D,), jnp.float32), 'ln3_b': jnp.zeros((D,), jnp.float32), 'a1_wq': nrm(ks[2], (D, INNER)), 'a1_wk': nrm(ks[3], (D, INNER)), 'a1_wv': nrm(ks[4], (D, INNER)), 'a1_wo': nrm(ks[5], (INNER, D)), 'a1_bo': jnp.zeros((D,), jnp.float32), 'a2_wq': nrm(ks[6], (D, INNER)), 'a2_wk': nrm(ks[7], (CTX_DIM, INNER)), 'a2_wv': nrm(ks[8], (CTX_DIM, INNER)), 'a2_wo': nrm(ks[9], (INNER, D)), 'a2_bo': jnp.zeros((D,), jnp.float32), 'ff_w1': nrm(ks[10], (D, D * MULT * 2)), 'ff_b1': jnp.zeros((D * MULT * 2,), jnp.float32), 'ff_w2': nrm(ks[11], (D * MULT, D)), 'ff_b2': jnp.zeros((D,), jnp.float32)}
    _L2_xattn_all = _L2_xattn_setup()
    _L2_xattn_in = {k: v for k, v in _L2_xattn_all.items() if k in ('ln1_g', 'ln1_b', 'ln2_g', 'ln2_b', 'ln3_g', 'ln3_b', 'a1_wq', 'a1_wk', 'a1_wv', 'a1_wo', 'a1_bo', 'a2_wq', 'a2_wk', 'a2_wv', 'a2_wo', 'a2_bo', 'ff_w1', 'ff_b1', 'ff_w2', 'ff_b2')}
    del _L2_xattn_all

    def _L3_xattn_setup():
        import jax, jax.numpy as jnp
        import numpy as np
        LATENT = 128
        TEXT = 96
        HEADS = 16
        HEAD_DIM = LATENT // HEADS
        SCALE = HEAD_DIM ** (-0.5)
        LN_EPS = 1e-05
        key = jax.random.key(seed)
        ks = jax.random.split(key, 16)
        B, Tx, Txf = (4, 512, 32)

        def lin(k, fan_in, fan_out):
            bound = 1.0 / np.sqrt(fan_in)
            kw, kb = jax.random.split(k)
            W = jax.random.uniform(kw, (fan_in, fan_out), jnp.float32, -bound, bound)
            b = jax.random.uniform(kb, (fan_out,), jnp.float32, -bound, bound)
            return (W, b)
        Wq, bq = lin(ks[0], LATENT, LATENT)
        Wk, bk = lin(ks[1], TEXT, LATENT)
        Wv, bv = lin(ks[2], TEXT, LATENT)
        Wo, bo = lin(ks[3], LATENT, LATENT)
        W1, b1 = lin(ks[4], LATENT, 4 * LATENT)
        W2, b2 = lin(ks[5], 4 * LATENT, LATENT)
        return {'x': jax.random.normal(ks[6], (B, Tx, LATENT), jnp.float32), 'xf': jax.random.normal(ks[7], (B, Txf, TEXT), jnp.float32), 'Wq': Wq, 'bq': bq, 'Wk': Wk, 'bk': bk, 'Wv': Wv, 'bv': bv, 'Wo': Wo, 'bo': bo, 'ln_g': jnp.ones((LATENT,), jnp.float32), 'ln_b': jnp.zeros((LATENT,), jnp.float32), 'W1': W1, 'b1': b1, 'W2': W2, 'b2': b2}
    _L3_xattn_all = _L3_xattn_setup()
    _L3_xattn_in = {k: v for k, v in _L3_xattn_all.items() if k in ('Wq', 'bq', 'Wk', 'bk', 'Wv', 'bv', 'Wo', 'bo', 'ln_g', 'ln_b', 'W1', 'b1', 'W2', 'b2')}
    del _L3_xattn_all
    return {'x': x, 'ctx_768': ctx_768, 'mask_BxS_bf0': mask_BxS_bf0, 'mask_BxS2_bf0': mask_BxS2_bf0, 'L0_xattn_Wq1': _L0_xattn_in['Wq1'], 'L0_xattn_Wk1': _L0_xattn_in['Wk1'], 'L0_xattn_Wv1': _L0_xattn_in['Wv1'], 'L0_xattn_Wo1': _L0_xattn_in['Wo1'], 'L0_xattn_bo1': _L0_xattn_in['bo1'], 'L0_xattn_Wq2': _L0_xattn_in['Wq2'], 'L0_xattn_Wk2': _L0_xattn_in['Wk2'], 'L0_xattn_Wv2': _L0_xattn_in['Wv2'], 'L0_xattn_Wo2': _L0_xattn_in['Wo2'], 'L0_xattn_bo2': _L0_xattn_in['bo2'], 'L0_xattn_Wp': _L0_xattn_in['Wp'], 'L0_xattn_bp': _L0_xattn_in['bp'], 'L0_xattn_Wf': _L0_xattn_in['Wf'], 'L0_xattn_bf': _L0_xattn_in['bf'], 'L0_xattn_g1': _L0_xattn_in['g1'], 'L0_xattn_b1': _L0_xattn_in['b1'], 'L0_xattn_g2': _L0_xattn_in['g2'], 'L0_xattn_b2': _L0_xattn_in['b2'], 'L0_xattn_g3': _L0_xattn_in['g3'], 'L0_xattn_b3': _L0_xattn_in['b3'], 'L1_xattn_ln1_w': _L1_xattn_in['ln1_w'], 'L1_xattn_ln1_b': _L1_xattn_in['ln1_b'], 'L1_xattn_qkv_w': _L1_xattn_in['qkv_w'], 'L1_xattn_qkv_b': _L1_xattn_in['qkv_b'], 'L1_xattn_proj_w': _L1_xattn_in['proj_w'], 'L1_xattn_proj_b': _L1_xattn_in['proj_b'], 'L1_xattn_ln2_w': _L1_xattn_in['ln2_w'], 'L1_xattn_ln2_b': _L1_xattn_in['ln2_b'], 'L1_xattn_q_w': _L1_xattn_in['q_w'], 'L1_xattn_q_b': _L1_xattn_in['q_b'], 'L1_xattn_k_w': _L1_xattn_in['k_w'], 'L1_xattn_k_b': _L1_xattn_in['k_b'], 'L1_xattn_v_w': _L1_xattn_in['v_w'], 'L1_xattn_v_b': _L1_xattn_in['v_b'], 'L1_xattn_out_w': _L1_xattn_in['out_w'], 'L1_xattn_out_b': _L1_xattn_in['out_b'], 'L1_xattn_ln3_w': _L1_xattn_in['ln3_w'], 'L1_xattn_ln3_b': _L1_xattn_in['ln3_b'], 'L1_xattn_mlp1_w': _L1_xattn_in['mlp1_w'], 'L1_xattn_mlp1_b': _L1_xattn_in['mlp1_b'], 'L1_xattn_mlp2_w': _L1_xattn_in['mlp2_w'], 'L1_xattn_mlp2_b': _L1_xattn_in['mlp2_b'], 'L2_xattn_ln1_g': _L2_xattn_in['ln1_g'], 'L2_xattn_ln1_b': _L2_xattn_in['ln1_b'], 'L2_xattn_ln2_g': _L2_xattn_in['ln2_g'], 'L2_xattn_ln2_b': _L2_xattn_in['ln2_b'], 'L2_xattn_ln3_g': _L2_xattn_in['ln3_g'], 'L2_xattn_ln3_b': _L2_xattn_in['ln3_b'], 'L2_xattn_a1_wq': _L2_xattn_in['a1_wq'], 'L2_xattn_a1_wk': _L2_xattn_in['a1_wk'], 'L2_xattn_a1_wv': _L2_xattn_in['a1_wv'], 'L2_xattn_a1_wo': _L2_xattn_in['a1_wo'], 'L2_xattn_a1_bo': _L2_xattn_in['a1_bo'], 'L2_xattn_a2_wq': _L2_xattn_in['a2_wq'], 'L2_xattn_a2_wk': _L2_xattn_in['a2_wk'], 'L2_xattn_a2_wv': _L2_xattn_in['a2_wv'], 'L2_xattn_a2_wo': _L2_xattn_in['a2_wo'], 'L2_xattn_a2_bo': _L2_xattn_in['a2_bo'], 'L2_xattn_ff_w1': _L2_xattn_in['ff_w1'], 'L2_xattn_ff_b1': _L2_xattn_in['ff_b1'], 'L2_xattn_ff_w2': _L2_xattn_in['ff_w2'], 'L2_xattn_ff_b2': _L2_xattn_in['ff_b2'], 'L3_xattn_Wq': _L3_xattn_in['Wq'], 'L3_xattn_bq': _L3_xattn_in['bq'], 'L3_xattn_Wk': _L3_xattn_in['Wk'], 'L3_xattn_bk': _L3_xattn_in['bk'], 'L3_xattn_Wv': _L3_xattn_in['Wv'], 'L3_xattn_bv': _L3_xattn_in['bv'], 'L3_xattn_Wo': _L3_xattn_in['Wo'], 'L3_xattn_bo': _L3_xattn_in['bo'], 'L3_xattn_ln_g': _L3_xattn_in['ln_g'], 'L3_xattn_ln_b': _L3_xattn_in['ln_b'], 'L3_xattn_W1': _L3_xattn_in['W1'], 'L3_xattn_b1': _L3_xattn_in['b1'], 'L3_xattn_W2': _L3_xattn_in['W2'], 'L3_xattn_b2': _L3_xattn_in['b2']}

def reference(x, ctx_768, mask_BxS_bf0, mask_BxS2_bf0, L0_xattn_Wq1, L0_xattn_Wk1, L0_xattn_Wv1, L0_xattn_Wo1, L0_xattn_bo1, L0_xattn_Wq2, L0_xattn_Wk2, L0_xattn_Wv2, L0_xattn_Wo2, L0_xattn_bo2, L0_xattn_Wp, L0_xattn_bp, L0_xattn_Wf, L0_xattn_bf, L0_xattn_g1, L0_xattn_b1, L0_xattn_g2, L0_xattn_b2, L0_xattn_g3, L0_xattn_b3, L1_xattn_ln1_w, L1_xattn_ln1_b, L1_xattn_qkv_w, L1_xattn_qkv_b, L1_xattn_proj_w, L1_xattn_proj_b, L1_xattn_ln2_w, L1_xattn_ln2_b, L1_xattn_q_w, L1_xattn_q_b, L1_xattn_k_w, L1_xattn_k_b, L1_xattn_v_w, L1_xattn_v_b, L1_xattn_out_w, L1_xattn_out_b, L1_xattn_ln3_w, L1_xattn_ln3_b, L1_xattn_mlp1_w, L1_xattn_mlp1_b, L1_xattn_mlp2_w, L1_xattn_mlp2_b, L2_xattn_ln1_g, L2_xattn_ln1_b, L2_xattn_ln2_g, L2_xattn_ln2_b, L2_xattn_ln3_g, L2_xattn_ln3_b, L2_xattn_a1_wq, L2_xattn_a1_wk, L2_xattn_a1_wv, L2_xattn_a1_wo, L2_xattn_a1_bo, L2_xattn_a2_wq, L2_xattn_a2_wk, L2_xattn_a2_wv, L2_xattn_a2_wo, L2_xattn_a2_bo, L2_xattn_ff_w1, L2_xattn_ff_b1, L2_xattn_ff_w2, L2_xattn_ff_b2, L3_xattn_Wq, L3_xattn_bq, L3_xattn_Wk, L3_xattn_bk, L3_xattn_Wv, L3_xattn_bv, L3_xattn_Wo, L3_xattn_bo, L3_xattn_ln_g, L3_xattn_ln_b, L3_xattn_W1, L3_xattn_b1, L3_xattn_W2, L3_xattn_b2):
    import jax
    import jax.numpy as jnp

    def _L0_xattn_ref(x, context, Wq1, Wk1, Wv1, Wo1, bo1, Wq2, Wk2, Wv2, Wo2, bo2, Wp, bp, Wf, bf, g1, b1, g2, b2, g3, b3):
        import jax, jax.numpy as jnp
        import numpy as np
        HEADS = 16
        D_HEAD = 64
        EPS = 1e-05

        def _ln(x, g, b):
            m = jnp.mean(x, axis=-1, keepdims=True)
            v = jnp.var(x, axis=-1, keepdims=True)
            return (x - m) * jax.lax.rsqrt(v + EPS) * g + b

        def _attn(xq, xc, Wq, Wk, Wv, Wo, bo):
            B, N, _ = xq.shape
            S = xc.shape[1]
            q = (xq @ Wq).reshape(B, N, HEADS, D_HEAD)
            k = (xc @ Wk).reshape(B, S, HEADS, D_HEAD)
            v = (xc @ Wv).reshape(B, S, HEADS, D_HEAD)
            scale = D_HEAD ** (-0.5)
            scores = jnp.einsum('bnhd,bshd->bhns', q, k) * scale
            attn = jax.nn.softmax(scores, axis=-1)
            out = jnp.einsum('bhns,bshd->bnhd', attn, v).reshape(B, N, HEADS * D_HEAD)
            return out @ Wo + bo

        def _geglu_ff(x, Wp, bp, Wf, bf):
            h = x @ Wp + bp
            a, gate = jnp.split(h, 2, axis=-1)
            return a * jax.nn.gelu(gate, approximate=False) @ Wf + bf
        x = _attn(_ln(x, g1, b1), _ln(x, g1, b1), Wq1, Wk1, Wv1, Wo1, bo1) + x
        x = _attn(_ln(x, g2, b2), context, Wq2, Wk2, Wv2, Wo2, bo2) + x
        x = _geglu_ff(_ln(x, g3, b3), Wp, bp, Wf, bf) + x
        return x

    def _L1_xattn_ref(x, enc, tgt_key_padding_mask, enc_padding_mask, ln1_w, ln1_b, qkv_w, qkv_b, proj_w, proj_b, ln2_w, ln2_b, q_w, q_b, k_w, k_b, v_w, v_b, out_w, out_b, ln3_w, ln3_b, mlp1_w, mlp1_b, mlp2_w, mlp2_b):
        import jax, jax.numpy as jnp
        import numpy as np
        D_DEC, D_ENC, H, D_MLP = (128, 96, 16, 512)
        HD = D_DEC // H

        def _layernorm(x, w, b, eps=1e-05):
            m = x.mean(-1, keepdims=True)
            v = ((x - m) ** 2).mean(-1, keepdims=True)
            return (x - m) / jnp.sqrt(v + eps) * w + b

        def _decoder_block(x, enc, tgt_mask, enc_mask, ln1_w, ln1_b, qkv_w, qkv_b, proj_w, proj_b, ln2_w, ln2_b, q_w, q_b, k_w, k_b, v_w, v_b, out_w, out_b, ln3_w, ln3_b, mlp1_w, mlp1_b, mlp2_w, mlp2_b):
            B, T, C = x.shape
            S = enc.shape[1]
            scale = HD ** (-0.5)
            neg = jnp.asarray(-jnp.inf, x.dtype)
            h = _layernorm(x, ln1_w, ln1_b)
            qkv = (h @ qkv_w + qkv_b).reshape(B, T, 3, H, HD)
            q, k, v = [qkv[:, :, i].transpose(0, 2, 1, 3) for i in range(3)]
            attn = jnp.einsum('bhtd,bhsd->bhts', q, k) * scale
            causal = jnp.triu(jnp.ones((T, T), bool), 1)
            attn = jnp.where(causal[None, None], neg, attn)
            attn = jnp.where(tgt_mask[:, None, None, :], neg, attn)
            attn = jax.nn.softmax(attn, axis=-1)
            sa = jnp.einsum('bhts,bhsd->bhtd', attn, v).transpose(0, 2, 1, 3).reshape(B, T, C)
            x = x + sa @ proj_w + proj_b
            h = _layernorm(x, ln2_w, ln2_b)
            q = (h @ q_w + q_b).reshape(B, T, H, HD).transpose(0, 2, 1, 3)
            k = (enc @ k_w + k_b).reshape(B, S, H, HD).transpose(0, 2, 1, 3)
            v = (enc @ v_w + v_b).reshape(B, S, H, HD).transpose(0, 2, 1, 3)
            attn = jnp.einsum('bhtd,bhsd->bhts', q, k) * scale
            attn = jnp.where(enc_mask[:, None, None, :], neg, attn)
            attn = jax.nn.softmax(attn, axis=-1)
            ca = jnp.einsum('bhts,bhsd->bhtd', attn, v).transpose(0, 2, 1, 3).reshape(B, T, C)
            x = x + ca @ out_w + out_b
            h = _layernorm(x, ln3_w, ln3_b)
            h = jax.nn.gelu(h @ mlp1_w + mlp1_b, approximate=False)
            x = x + h @ mlp2_w + mlp2_b
            return x
        return _decoder_block(x, enc, tgt_key_padding_mask, enc_padding_mask, ln1_w, ln1_b, qkv_w, qkv_b, proj_w, proj_b, ln2_w, ln2_b, q_w, q_b, k_w, k_b, v_w, v_b, out_w, out_b, ln3_w, ln3_b, mlp1_w, mlp1_b, mlp2_w, mlp2_b)

    def _L2_xattn_ref(x, context, ln1_g, ln1_b, ln2_g, ln2_b, ln3_g, ln3_b, a1_wq, a1_wk, a1_wv, a1_wo, a1_bo, a2_wq, a2_wk, a2_wv, a2_wo, a2_bo, ff_w1, ff_b1, ff_w2, ff_b2):
        import jax, jax.numpy as jnp
        import numpy as np
        B, S, D = (4, 256, 128)
        CTX_LEN, CTX_DIM = (77, 96)
        H, DH = (16, 64)
        INNER = H * DH
        MULT = 4
        EPS = 1e-05

        def _layernorm(x, g, b):
            mu = jnp.mean(x, axis=-1, keepdims=True)
            var = jnp.var(x, axis=-1, keepdims=True)
            return (x - mu) * jax.lax.rsqrt(var + EPS) * g + b

        def _attn(xq, xkv, wq, wk, wv, wo, bo):
            b, sq, _ = xq.shape
            sk = xkv.shape[1]
            q = (xq @ wq).reshape(b, sq, H, DH)
            k = (xkv @ wk).reshape(b, sk, H, DH)
            v = (xkv @ wv).reshape(b, sk, H, DH)
            score = jnp.einsum('bqhd,bkhd->bhqk', q, k) * DH ** (-0.5)
            w = jax.nn.softmax(score, axis=-1)
            o = jnp.einsum('bhqk,bkhd->bqhd', w, v).reshape(b, sq, INNER)
            return o @ wo + bo

        def _block(x, context, ln1_g, ln1_b, ln2_g, ln2_b, ln3_g, ln3_b, a1_wq, a1_wk, a1_wv, a1_wo, a1_bo, a2_wq, a2_wk, a2_wv, a2_wo, a2_bo, ff_w1, ff_b1, ff_w2, ff_b2):
            x = _attn(_layernorm(x, ln1_g, ln1_b), _layernorm(x, ln1_g, ln1_b), a1_wq, a1_wk, a1_wv, a1_wo, a1_bo) + x
            x = _attn(_layernorm(x, ln2_g, ln2_b), context, a2_wq, a2_wk, a2_wv, a2_wo, a2_bo) + x
            h = _layernorm(x, ln3_g, ln3_b) @ ff_w1 + ff_b1
            u, gate = jnp.split(h, 2, axis=-1)
            x = u * jax.nn.gelu(gate, approximate=False) @ ff_w2 + ff_b2 + x
            return x
        return _block(x, context, ln1_g, ln1_b, ln2_g, ln2_b, ln3_g, ln3_b, a1_wq, a1_wk, a1_wv, a1_wo, a1_bo, a2_wq, a2_wk, a2_wv, a2_wo, a2_bo, ff_w1, ff_b1, ff_w2, ff_b2)

    def _L3_xattn_ref(x, xf, Wq, bq, Wk, bk, Wv, bv, Wo, bo, ln_g, ln_b, W1, b1, W2, b2):
        import jax, jax.numpy as jnp
        import numpy as np
        LATENT = 128
        TEXT = 96
        HEADS = 16
        HEAD_DIM = LATENT // HEADS
        SCALE = HEAD_DIM ** (-0.5)
        LN_EPS = 1e-05
        B, Tx, D = x.shape
        Txf = xf.shape[1]
        q = (x @ Wq + bq).reshape(B, Tx, HEADS, HEAD_DIM).transpose(0, 2, 1, 3)
        k = (xf @ Wk + bk).reshape(B, Txf, HEADS, HEAD_DIM).transpose(0, 2, 1, 3)
        v = (xf @ Wv + bv).reshape(B, Txf, HEADS, HEAD_DIM).transpose(0, 2, 1, 3)
        scores = jnp.einsum('bhqd,bhkd->bhqk', q * SCALE, k)
        probs = jax.nn.softmax(scores, axis=-1)
        attn = jnp.einsum('bhqk,bhkd->bhqd', probs, v)
        out = attn.transpose(0, 2, 1, 3).reshape(B, Tx, D)
        out = out @ Wo + bo
        mu = jnp.mean(out, axis=-1, keepdims=True)
        var = jnp.var(out, axis=-1, keepdims=True)
        h = (out - mu) * jax.lax.rsqrt(var + LN_EPS) * ln_g + ln_b
        h = jax.nn.gelu(h @ W1 + b1, approximate=False)
        ffn = h @ W2 + b2
        out = out + ffn
        return x + out
    x = _L0_xattn_ref(x, ctx_768, L0_xattn_Wq1, L0_xattn_Wk1, L0_xattn_Wv1, L0_xattn_Wo1, L0_xattn_bo1, L0_xattn_Wq2, L0_xattn_Wk2, L0_xattn_Wv2, L0_xattn_Wo2, L0_xattn_bo2, L0_xattn_Wp, L0_xattn_bp, L0_xattn_Wf, L0_xattn_bf, L0_xattn_g1, L0_xattn_b1, L0_xattn_g2, L0_xattn_b2, L0_xattn_g3, L0_xattn_b3)
    x = _L1_xattn_ref(x, ctx_768, mask_BxS_bf0, mask_BxS2_bf0, L1_xattn_ln1_w, L1_xattn_ln1_b, L1_xattn_qkv_w, L1_xattn_qkv_b, L1_xattn_proj_w, L1_xattn_proj_b, L1_xattn_ln2_w, L1_xattn_ln2_b, L1_xattn_q_w, L1_xattn_q_b, L1_xattn_k_w, L1_xattn_k_b, L1_xattn_v_w, L1_xattn_v_b, L1_xattn_out_w, L1_xattn_out_b, L1_xattn_ln3_w, L1_xattn_ln3_b, L1_xattn_mlp1_w, L1_xattn_mlp1_b, L1_xattn_mlp2_w, L1_xattn_mlp2_b)
    x = _L2_xattn_ref(x, ctx_768, L2_xattn_ln1_g, L2_xattn_ln1_b, L2_xattn_ln2_g, L2_xattn_ln2_b, L2_xattn_ln3_g, L2_xattn_ln3_b, L2_xattn_a1_wq, L2_xattn_a1_wk, L2_xattn_a1_wv, L2_xattn_a1_wo, L2_xattn_a1_bo, L2_xattn_a2_wq, L2_xattn_a2_wk, L2_xattn_a2_wv, L2_xattn_a2_wo, L2_xattn_a2_bo, L2_xattn_ff_w1, L2_xattn_ff_b1, L2_xattn_ff_w2, L2_xattn_ff_b2)
    x = _L3_xattn_ref(x, ctx_768, L3_xattn_Wq, L3_xattn_bq, L3_xattn_Wk, L3_xattn_bk, L3_xattn_Wv, L3_xattn_bv, L3_xattn_Wo, L3_xattn_bo, L3_xattn_ln_g, L3_xattn_ln_b, L3_xattn_W1, L3_xattn_b1, L3_xattn_W2, L3_xattn_b2)
    return x

_drawn_inputs = setup_inputs


def setup_inputs(seed=0):
    import zlib

    import numpy as np

    out = dict(_drawn_inputs(seed))
    spreads = {'L0_xattn_bo1': (0.0, 0.1),
     'L0_xattn_bo2': (0.0, 0.1),
     'L0_xattn_bp': (0.0, 0.1),
     'L0_xattn_bf': (0.0, 0.1),
     'L0_xattn_g1': (1.0, 0.2),
     'L0_xattn_b1': (0.0, 0.1),
     'L0_xattn_g2': (1.0, 0.2),
     'L0_xattn_b2': (0.0, 0.379),
     'L0_xattn_g3': (1.0, 0.2),
     'L0_xattn_b3': (0.0, 0.1),
     'L1_xattn_ln1_w': (1.0, 0.6),
     'L1_xattn_ln1_b': (0.0, 0.354),
     'L1_xattn_ln2_w': (1.0, 0.6),
     'L1_xattn_ln2_b': (0.0, 0.8),
     'L1_xattn_ln3_w': (1.0, 0.6),
     'L1_xattn_ln3_b': (0.0, 0.595),
     'L2_xattn_ln1_g': (1.0, 0.6),
     'L2_xattn_ln1_b': (0.0, 0.8),
     'L2_xattn_ln2_g': (1.0, 0.6),
     'L2_xattn_ln2_b': (0.0, 0.8),
     'L2_xattn_ln3_g': (1.0, 0.6),
     'L2_xattn_ln3_b': (0.0, 0.8),
     'L2_xattn_a1_bo': (0.0, 0.1),
     'L2_xattn_a2_bo': (0.0, 0.1),
     'L2_xattn_ff_b1': (0.0, 0.8),
     'L2_xattn_ff_b2': (0.0, 0.55),
     'L3_xattn_ln_g': (1.0, 0.6),
     'L3_xattn_ln_b': (0.0, 2.0)}
    factors = {'L1_xattn_qkv_b': 2.739,
     'L1_xattn_q_w': 3.73,
     'L1_xattn_q_b': 8.0,
     'L1_xattn_k_w': 3.64,
     'L1_xattn_k_b': 64.0,
     'L1_xattn_mlp1_b': 4.47,
     'L1_xattn_mlp2_b': 3.08,
     'L2_xattn_a1_wq': 8.0,
     'L2_xattn_a1_wk': 8.0,
     'L2_xattn_a2_wq': 8.0,
     'L2_xattn_a2_wk': 8.0,
     'L2_xattn_ff_w1': 4.981,
     'L2_xattn_ff_w2': 4.891,
     'L3_xattn_bq': 64.0,
     'L3_xattn_bk': 64.0,
     'L3_xattn_b1': 20.562,
     'L3_xattn_b2': 15.789,
     'L3_xattn_bv': 7.643,
     'L3_xattn_bo': 4.185}
    for name, (base, spread) in spreads.items():
        noise = np.random.default_rng([zlib.crc32(name.encode()), seed]).standard_normal(out[name].shape)
        drawn = base * np.exp(spread * noise) if base else spread * noise
        out[name] = jnp.asarray(drawn.astype(out[name].dtype))
    for name, factor in factors.items():
        out[name] = (out[name] * factor).astype(out[name].dtype)
    return out
```

```python
from contextlib import ExitStack

import numpy as np

import concourse.bass as bass
from concourse import mybir

F32 = mybir.dt.float32
F32R = mybir.dt.float32r
BF16 = mybir.dt.bfloat16
U8 = mybir.dt.uint8
ALU = mybir.AluOpType
ACT = mybir.ActivationFunctionType
AX = mybir.AxisListType

B, S, D, C = 8, 256, 128, 96
HEADS, DH, DS = 16, 64, 8
INNER = HEADS * DH
FF = 512
P = 128
NT = S // P
SLOTS = 2
TURNS = B // SLOTS
EPS = 1e-5
BIG = -1.0e38
SMALL_SCALE = float(DS) ** -0.5
BIG_SCALE = float(DH) ** -0.5

PHASES = [(0, True, True), (0, False, True), (1, True, False), (1, False, False),
          (2, True, True), (2, False, True), (3, False, False)]
BIGS = [p for p, ph in enumerate(PHASES) if ph[2]]
SMALLS = [p for p, ph in enumerate(PHASES) if not ph[2]]
QUADS = HEADS // 4
LAYERS = 4


def rows_of(p):
    return D if PHASES[p][1] else C


def column_names():
    names = []
    for ln in range(10):
        names += [f"g{ln}", f"b{ln}"]
    for layer in range(LAYERS):
        names += [f"ffb{layer}_{j}" for j in range(8 if layer in (0, 2) else 4)]
    for p in SMALLS:
        for kind in ("qb", "qmb", "kb", "kmb"):
            names += [f"{kind}{p}_{g}" for g in range(QUADS)]
    names += ["mq", "mk", "neghalf0", "neghalf1"]
    return names


def row_names():
    return [f"yo{p}" for p in range(7)] + [f"fo{l}" for l in range(LAYERS)] + [f"vb{p}" for p in SMALLS]


COLS = {n: i for i, n in enumerate(column_names())}
ROWS = {n: i for i, n in enumerate(row_names())}
ROW_W = (len(ROWS) + 3) // 4


class Tally:

    def __init__(self, sem, keys):
        self.sem, self.at, self.total = sem, {k: i + 1 for i, k in enumerate(keys)}, len(keys)
        assert len(self.at) == self.total

    def after(self, key, turn):
        return self.sem, turn * self.total + self.at[key]

    def last(self, keys):
        return max(keys, key=self.at.get)


FF_A_STEP = 2
HEAD_N = len(PHASES) * SLOTS * HEADS


def head(n):
    return n // (SLOTS * HEADS), n // HEADS % SLOTS, n % HEADS


def first_head(p, s):
    return (p * SLOTS + s) * HEADS


LN_BEFORE = {0: 0, 1: 1, 2: 3, 3: 4, 4: 6, 5: 7}
LN_FF = {0: 2, 1: 5, 2: 8, 3: 9}


def plan():
    steps = {}
    pieces = []

    def put(step, kind, **kw):
        piece = dict(kind=kind, id=len(pieces), step=step, **kw)
        pieces.append(piece)
        steps.setdefault(step, []).append(piece)
        return piece

    def inputs_of(p, s, at, h):
        if PHASES[p][2]:
            order = [("v", j) for j in range(4)]
        else:
            order = [("q", 0), ("k", 0), ("v", 0), ("v", 1), ("q", 1), ("k", 1)]
        for kind, j in order:
            put(at, kind, p=p, s=s, j=j, h=h)
            at += 1

    def after_phase(p, s, at):
        layer = PHASES[p][0]
        put(at, "y", p=p, s=s)
        x = put(at + 1, "xn", p=p, s=s, of="y")
        last = p + 1 == len(PHASES) or PHASES[p + 1][0] != layer
        at += 2
        if last:
            h = put(at, "h", s=s, ln=LN_FF[layer], x=x)
            n = 4 if layer in (0, 2) else 2
            ffs = [put(at + 1 + j // FF_A_STEP, "ff", p=p, s=s, layer=layer, j=j, h=h) for j in range(n)]
            at += 1 + (n + FF_A_STEP - 1) // FF_A_STEP
            f = put(at, "f", p=p, s=s, layer=layer, ffs=ffs)
            at += 1
            if p + 1 == len(PHASES):
                return
            if p + 1 in LN_BEFORE:
                x = put(at, "xn", p=p, s=s, of="f")
                at += 1
        if p + 1 in LN_BEFORE:
            h = put(at, "h", s=s, ln=LN_BEFORE[p + 1], x=x)
        else:
            h = put(at, "h", s=s, ln=None, x=f)
        inputs_of(p + 1, s, at + 1, h)

    def start(s, at):
        put(at, "in", s=s)
        x = put(at + 1, "xn", p=-1, s=s, of="in")
        h = put(at + 2, "h", s=s, ln=LN_BEFORE[0], x=x)
        inputs_of(0, s, at + 3, h)

    start(0, -7)
    start(1, 0)
    for p in range(len(PHASES)):
        for s in range(SLOTS):
            after_phase(p, s, first_head(p, s) + HEADS + 5)
    order = [q for i in sorted(steps) for q in steps[i]]
    return steps, order


STEPS, ORDER = plan()
FIRST_STEP, LAST_STEP = min(STEPS), max(max(STEPS) + 1, HEAD_N + 6)
AUX_KINDS = ("y", "h", "ff", "f", "q", "k", "v")
AUX = [q for q in ORDER if q["kind"] in AUX_KINDS]
for _i, _q in enumerate(AUX):
    _q["aux"] = _i


def dve_parts(q):
    k = q["kind"]
    if k == "in":
        return ["x", "clo", "mask"] + ["st0", "st1", "mv0", "mv1", "ve"]
    if k == "y":
        return ["x"] + ["st0", "st1", "mv0", "mv1", "ve"]
    if k == "f":
        if q["p"] + 1 == len(PHASES) or q["p"] + 1 not in LN_BEFORE:
            return ["x"]
        return ["x"] + ["st0", "st1", "mv0", "mv1", "ve"]
    if k == "xn":
        return ["xn0", "xn1"] + (["res"] if q["p"] == 6 else [])
    if k == "h":
        return ["hi", "lo"]
    if k == "ff":
        return ["ff"] if q["layer"] in (0, 2) else []
    if k in "qk":
        return ["0", "1"]
    return []


def act_parts(q):
    k = q["kind"]
    if k == "in":
        return ["chi"]
    if k == "h":
        return ["h"]
    if k == "ff":
        return ["ff"] if q["layer"] in (0, 2) else ["ff0", "ff1"]
    if k in ("q", "k"):
        return ["0", "1"]
    if k == "v":
        return ["v"]
    return []


def group_of(n):
    p, s, h = head(n)
    return (p, s, h // (2 if PHASES[p][2] else 4))


GROUPS = list(dict.fromkeys(group_of(n) for n in range(HEAD_N)))
GROUP_LAST = {group_of(n): n for n in range(HEAD_N)}
BIG_HEADS = [n for n in range(HEAD_N) if PHASES[head(n)[0]][2]]


def find(kind, **kw):
    got = [q for q in ORDER if q["kind"] == kind and all(q.get(k) == v for k, v in kw.items())]
    assert len(got) == 1, (kind, kw, len(got))
    return got[0]


def build(nc, a, out):
    with ExitStack() as ctx:
        def sb(name, shape, dt=F32):
            return ctx.enter_context(nc.sbuf_tensor(name, shape, dt))

        def sem(name):
            return ctx.enter_context(nc.semaphore(name))

        g_ring = [sb(f"g_ring{i}", [P, 2, HEADS, P], F32R) for i in range(2)]
        wv_ring = sb("wv_ring", [P, 2, INNER], F32R)
        wo_ring = sb("wo_ring", [P, HEADS // 2, D])
        w_up = {l: sb(f"w_up{l}", [P, 2, 2 * FF if l in (0, 2) else FF], F32R) for l in range(LAYERS)}
        w_down = {l: sb(f"w_down{l}", [P, FF // P, D]) for l in range(LAYERS)}
        wq = {p: sb(f"wq{p}", [P, 2, QUADS * P], F32R) for p in SMALLS}
        wk = {p: sb(f"wk{p}", [P, 2, QUADS * P], F32R) for p in SMALLS}
        wv = {p: sb(f"wv{p}", [P, 2, QUADS * P], F32R) for p in SMALLS}
        wo = {p: sb(f"wo{p}", [P, QUADS, D]) for p in SMALLS}
        cols = sb("cols", [P, len(COLS)])
        rows = sb("rows", [P, ROW_W, D])
        ident = sb("ident", [P, P])
        ones = sb("ones", [P, P])
        ident_bf = sb("ident_bf", [P, P], BF16)
        causal = sb("causal", [P, P], BF16)
        mask_rows = sb("mask_rows", [1, P], BF16)

        x = [sb(f"x{s}", [P, NT, D]) for s in range(SLOTS)]
        x_in = [sb(f"x_in{s}", [P, NT, D]) for s in range(SLOTS)]
        c_in = [sb(f"c_in{s}", [C, S]) for s in range(SLOTS)]
        m_in = [sb(f"m_in{s}", [1, 2, S], U8) for s in range(SLOTS)]
        mask = [sb(f"mask{s}", [1, 2, S], BF16) for s in range(SLOTS)]
        ht = [sb(f"ht{s}", [P, 2, S], F32R) for s in range(SLOTS)]
        ct = [sb(f"ct{s}", [C, 2, S], F32R) for s in range(SLOTS)]
        v = [sb(f"v{s}", [P, NT * INNER]) for s in range(SLOTS)]
        qs = [sb(f"qs{s}", [P, QUADS, S], F32R) for s in range(SLOTS)]
        ks = [sb(f"ks{s}", [P, QUADS, S], F32R) for s in range(SLOTS)]
        ot = sb("ot", [P, HEADS // 2, S])
        xn = sb("xn", [P, NT, D])
        side = [sb(f"side{i}", [P, 2 * S]) for i in range(2)]
        ft = sb("ft", [P, FF // P, S])
        x3 = sb("x3", [P, NT, D])
        stats = sb("stats", [P, NT, 6])
        mv = sb("mv", [P, NT, 2])
        ve = sb("ve", [P, NT])
        fence = sb("fence", [P, 1])
        rstd = sb("rstd", [P, NT])
        th = [sb(f"th{i}", [P, 2, S], F32R) for i in range(2)]
        pr = [sb(f"pr{i}", [P, NT, S]) for i in range(2)]
        pn = [sb(f"pn{i}", [P, NT, S]) for i in range(3)]
        pt = [sb(f"pt{i}", [P, NT * S]) for i in range(2)]
        negmax = sb("negmax", [P, 4, NT])
        raw_negmax = sb("raw_negmax", [P, 4, NT])
        den = sb("den", [P, 4, NT])
        rden = sb("rden", [P, 4, NT])

        ps_t = ctx.enter_context(nc.psum_tensor("ps_t", [P, 512], F32))
        ps_s = [ctx.enter_context(nc.psum_tensor(f"ps_s{i}", [P, NT, S], F32)) for i in range(2)]
        ps_p = ctx.enter_context(nc.psum_tensor("ps_p", [P, NT * S], F32))
        ps_o = [ctx.enter_context(nc.psum_tensor(f"ps_o{i}", [P, 512], F32)) for i in range(2)]
        ps_x = [ctx.enter_context(nc.psum_tensor(f"ps_x{i}", [P, 512], F32)) for i in range(2)]

        g_dram = nc.dram_tensor("g_scratch", [4, P, 2, HEADS, P], F32, kind="Internal").ap()
        wv_dram = nc.dram_tensor("wv_scratch", [4, P, 2, INNER], F32, kind="Internal").ap()

        CONST_OPS = 5
        SETUP_CONSTS = 6
        RESIDENT = SETUP_CONSTS + LAYERS + len(SMALLS)
        x_taken = sem("x_taken")

        const_in = sem("const_in")
        raw_in = [sem(f"raw_in{i}") for i in range(10)]
        raw_used = sem("raw_used")
        g_made = sem("g_made")
        g_hi = sem("g_hi")
        g_lo = sem("g_lo")
        const_done = sem("const_done")
        split_hi = sem("split_hi")
        g_out = [sem(f"g_out{i}") for i in range(4)]
        wv_out = [sem(f"wv_out{i}") for i in range(4)]
        xin = [sem(f"xin{s}") for s in range(SLOTS)]
        g_in = [sem(f"g_in{i}") for i in range(2)]
        wv_in = sem("wv_in")
        wo_in = sem("wo_in")
        out_done = sem("out_done")
        heads = list(range(HEAD_N))
        t_ready = Tally(sem("t_ready"), BIG_HEADS)
        s_ready = Tally(sem("s_ready"), heads)
        tr_ready = Tally(sem("tr_ready"), heads)
        o_ready = Tally(sem("o_ready"), heads)
        aux_ready = Tally(sem("aux_ready"), [q["id"] for q in AUX])
        thi_ready = Tally(sem("thi_ready"), BIG_HEADS)
        exp_ready = Tally(sem("exp_ready"), heads)
        o_kept = Tally(sem("o_kept"), GROUPS)
        act_side = Tally(sem("act_side"), [(q["id"], k) for q in ORDER for k in act_parts(q)])
        tlo_ready = Tally(sem("tlo_ready"), BIG_HEADS)
        raw_max = Tally(sem("raw_max"), [n for n in heads if PHASES[head(n)[0]][0] == 1])
        max_ready = Tally(sem("max_ready"), heads)
        rden_ready = Tally(sem("rden_ready"), heads)
        pt_ready = Tally(sem("pt_ready"), heads)
        dve_side = Tally(sem("dve_side"), [(q["id"], k) for q in ORDER for k in dve_parts(q)])
        pn_ready = Tally(sem("pn_ready"), heads)
        rstd_ready = Tally(sem("rstd_ready"),
                           [q["id"] for q in ORDER if "ve" in dve_parts(q)])

        def col(name):
            return cols[:, COLS[name]:COLS[name] + 1]

        def f32(ap):
            return ap.bitcast(F32)

        areas = [v[0][:, 0:1024], v[0][:, 1024:2048], v[1][:, 0:1024], v[1][:, 1024:2048],
                 ot[:, :, :].rearrange("p a b -> p (a b)")[:, 0:1024],
                 ot[:, :, :].rearrange("p a b -> p (a b)")[:, 1024:2048],
                 ft[:, :, :].rearrange("p a b -> p (a b)")]
        NA = len(areas)

        def wide(ap):
            return ap.rearrange("p a b -> p (a b)")

        jobs = []
        for i in (2, 3, 0, 1):
            jobs.append(dict(kind="g", i=i, src=[a[f"wqt{i}"], a[f"wkt{i}"]]))
            jobs.append(dict(kind="split", src=[a[f"wv{i}"]], scale=1.0, store=i))
        split_to = {2: (wide(qs[0][:, :, :]), wide(ks[0][:, :, :])),
                    3: (wide(qs[1][:, :, :]), wide(ks[1][:, :, :])),
                    0: (wv_ring[:, 0, :], wv_ring[:, 1, :]),
                    1: (wide(qs[0][:, :, :]), wide(ks[0][:, :, :]))}
        for j in jobs:
            if j["kind"] == "split":
                j["hi"], j["lo"] = split_to[j["store"]]
        for l in range(LAYERS):
            jobs.append(dict(kind="split", src=[a[f"w_up{l}"]], scale=1.0, store=None,
                             hi=w_up[l][:, 0, :], lo=w_up[l][:, 1, :]))
        for p in SMALLS:
            for nm, w, sc in (("wq", wq, SMALL_SCALE), ("wk", wk, 1.0), ("wv", wv, 1.0)):
                jobs.append(dict(kind="split", src=[a[f"{nm}{p}s"]], scale=sc, store=None,
                                 hi=w[p][:, 0, :], lo=w[p][:, 1, :]))
        uses = []
        for j, job in enumerate(jobs):
            job["areas"] = []
            for k, src in enumerate(job["src"]):
                job["areas"].append(len(uses))
                uses.append((j, k))
        banks_of = {}
        splits = []
        for j, job in enumerate(jobs):
            if job["kind"] == "g":
                banks_of[j] = [4 * len(banks_of) + k for k in range(4)]
            else:
                job["n"] = len(splits)
                splits.append(j)
        stores = [j for j, job in enumerate(jobs) if job["kind"] == "g" or job["store"] is not None]
        setup_banks = [ps_s[0], ps_s[1], ps_o[0], ps_o[1]]

        def raw(u, r, n):
            return areas[u % NA][0:r, 0:n]

        block = ctx.enter_context(nc.Block())

        @block.sync
        def _(sp):
            sp.dma_start(ident[:, :], a["ident"]).then_inc(const_in, 16)
            sp.dma_start(ones[:, :], a["ones"]).then_inc(const_in, 16)
            sp.dma_start(cols[:, :], a["cols"]).then_inc(const_in, 16)
            sp.dma_start(rows[:, :, :], a["rows"]).then_inc(const_in, 16)
            sp.dma_start(xn[:, :, :], a["masks"]).then_inc(const_in, 16)
            sp.dma_start(wide(pr[0][:, :, :]), a["bias_ones"]).then_inc(const_in, 16)
            done_stores = []

            def free_area(u):
                j = uses[u - NA][0]
                if jobs[j]["kind"] == "g":
                    sp.wait_ge(g_made, banks_of[j][-1] + 1)
                else:
                    sp.wait_ge(raw_used, jobs[j]["n"] + 1)

            def store(j):
                job = jobs[j]
                if job["kind"] == "g":
                    i, r = job["i"], rows_of(BIGS[job["i"]])
                    sp.wait_ge(g_lo, banks_of[j][-1] + 1)
                    sp.dma_start(g_dram[i][:, :, :, 0:r], f32(g_ring[i % 2][:, :, :, 0:r])).then_inc(g_out[i], 16)
                else:
                    i = job["store"]
                    r = rows_of(BIGS[i])
                    sp.wait_ge(raw_used, job["n"] + 1)
                    for k, part in enumerate(("hi", "lo")):
                        sp.dma_start(wv_dram[i][0:r, k, :], f32(job[part])[0:r, :]).then_inc(wv_out[i], 16)

            for u, (j, k) in enumerate(uses):
                if u >= NA:
                    jj = uses[u - NA][0]
                    while stores and stores[0] <= jj:
                        store(stores.pop(0))
                    free_area(u)
                src = jobs[j]["src"][k]
                r, n = src.shape
                sp.dma_start(raw(u, r, n), src).then_inc(raw_in[u % NA], 16)
                if u == 3:
                    for s in range(SLOTS):
                        pass
            while stores:
                store(stores.pop(0))
            for l in range(LAYERS):
                sp.dma_start(w_down[l][:, :, :], a[f"w_down{l}"]).then_inc(const_in, 16)
            for p in SMALLS:
                sp.dma_start(wo[p][:, :, :], a[f"wo{p}s"]).then_inc(const_in, 16)
            for i in range(4):
                sp.wait_ge(g_out[i], 16)
                sp.wait_ge(wv_out[i], 32)
            sp.dma_start(wo_ring[:, :, :], a["wo0"]).then_inc(wo_in, 16)
            sp.sem_inc(g_in[0], 16)
            sp.sem_inc(g_in[1], 16)
            sp.sem_inc(wv_in, 16)
            sp.sem_inc(out_done, 16)
            sp.sem_inc(x_taken, 1)

            with sp.Fori(0, TURNS) as turn:
                for s in range(SLOTS):
                    sp.wait_ge(x_taken, turn * SLOTS + s + 1)
                    b = turn * SLOTS + s
                    sp.dma_start(x_in[s][:, :, :], a["x"][bass.ds(b, 1)].rearrange("o p t d -> (o p) t d")).then_inc(xin[s], 16)
                    sp.dma_start(c_in[s][:, :], a["c"][bass.ds(b, 1)].rearrange("o p t -> (o p) t")).then_inc(xin[s], 16)
                    sp.dma_start(m_in[s][:, :, :], a["m"][bass.ds(b, 1)]).then_inc(xin[s], 16)
                for i in range(4):
                    nxt = (i + 1) % 4
                    p = BIGS[i]
                    sp.wait_ge(*aux_ready.after(find("v", p=p, s=1, j=3)["id"], turn))
                    r = rows_of(BIGS[nxt])
                    sp.dma_start(f32(wv_ring[0:r, :, :]), wv_dram[nxt][0:r]).then_inc(wv_in, 16)
                    sp.wait_ge(*t_ready.after(first_head(p, 1) + HEADS - 1, turn))
                    gi = (i + 2) % 4
                    r = rows_of(BIGS[gi])
                    sp.dma_start(f32(g_ring[i % 2][:, :, :, 0:r]), g_dram[gi][:, :, :, 0:r]).then_inc(g_in[i % 2], 16)
                    sp.wait_ge(*aux_ready.after(find("y", p=p, s=1)["id"], turn))
                    sp.dma_start(wo_ring[:, :, :], a[f"wo{nxt}"]).then_inc(wo_in, 16)
                for s in range(SLOTS):
                    sp.wait_ge(*dve_side.after((find("f", p=6, s=s)["id"], "x"), turn))
                    b = turn * SLOTS + s
                    sp.dma_start(out[bass.ds(b, 1)].rearrange("o p t d -> (o p) t d"), x[s][:, :, :]).then_inc(out_done, 16)
            sp.wait_ge(out_done, 16 * (B + 1))
            sp.wait_ge(g_in[0], 16 * (2 * TURNS + 1))
            sp.wait_ge(g_in[1], 16 * (2 * TURNS + 1))
            sp.wait_ge(wv_in, 16 * (4 * TURNS + 1))
            sp.wait_ge(wo_in, 16 * (4 * TURNS + 1))

        @block.tensor
        def _(pe):
            def three(o, w_hi, w_lo, m_hi, m_lo, stop=True):
                pe.matmul(o, w_hi, m_lo, start=True, stop=False)
                pe.matmul(o, w_lo, m_hi, start=False, stop=False)
                return pe.matmul(o, w_hi, m_hi, start=False, stop=stop)

            for j, job in enumerate(jobs):
                if job["kind"] != "g":
                    continue
                r = rows_of(BIGS[job["i"]])
                uq, uk = job["areas"]
                pe.wait_ge(raw_in[uq % NA], 16 * (uq // NA + 1))
                pe.wait_ge(raw_in[uk % NA], 16 * (uk // NA + 1))
                for half in range(2):
                    for par in range(2):
                        n = banks_of[j][2 * half + par]
                        if n >= 4:
                            pe.wait_ge(g_lo, n - 3)
                        for t in range(4):
                            pair = 4 * half + t
                            last = pe.matmul(
                                setup_banks[n % 4][:, :, :].rearrange("p a b -> p (a b)")[:, t * P:t * P + r]
                                if n % 4 < 2 else setup_banks[n % 4][:, t * P:t * P + r],
                                raw(uq, P, 1024)[64 * par:64 * par + 64, pair * P:(pair + 1) * P],
                                raw(uk, P, 8 * r)[64 * par:64 * par + 64, pair * r:(pair + 1) * r],
                                start=True, stop=True)
                        last.then_inc(g_made, 1)
            pe.wait_ge(const_in, 16 * RESIDENT)
            pe.wait_ge(raw_used, len(splits))
            pe.wait_ge(const_done, CONST_OPS)
            pe.wait_ge(g_lo, 16)

            with pe.Fori(0, TURNS) as turn:

                def source(q):
                    p, s = q["p"], q["s"]
                    if q["kind"] == "q" or PHASES[p][1]:
                        return ht[s], D
                    return ct[s], C

                def source_made(q):
                    p, s = q["p"], q["s"]
                    if q["kind"] == "q" or PHASES[p][1]:
                        return q["h"]["id"], "lo"
                    return find("in", s=s)["id"], "clo"

                def await_inputs(q):
                    kind = q["kind"]
                    by_dve, by_act = [], []
                    if q["aux"] >= 2:
                        before = AUX[q["aux"] - 2]
                        if dve_parts(before):
                            by_dve.append((before["id"], dve_parts(before)[-1]))
                        else:
                            by_act.append((before["id"], act_parts(before)[-1]))
                    if kind == "h":
                        by_dve.append((q["x"]["id"], "x" if q["ln"] is None else "xn1"))
                    elif kind == "ff":
                        by_dve.append((q["h"]["id"], "lo"))
                    elif kind == "f":
                        for ff in q["ffs"]:
                            if dve_parts(ff):
                                by_dve.append((ff["id"], "ff"))
                            else:
                                by_act.append((ff["id"], "ff1"))
                    else:
                        by_dve.append(source_made(q))
                    if by_dve:
                        pe.wait_ge(*dve_side.after(dve_side.last(by_dve), turn))
                    if by_act:
                        pe.wait_ge(*act_side.after(act_side.last(by_act), turn))

                def bias_row(o, name, stop=True):
                    i = ROWS[name]
                    r = 32 * (i % 4)
                    return pe.matmul(o, ones[r:r + 1, :], rows[r:r + 1, i // 4, :], start=False, stop=stop)

                def out_projection(q, part):
                    p, s = q["p"], q["s"]
                    groups = [g for g in GROUPS if g[:2] == (p, s)]
                    half = len(groups) // 2 * (part + 1)
                    if part == 0:
                        before = AUX[q["aux"] - 2]
                        if dve_parts(before):
                            pe.wait_ge(*dve_side.after((before["id"], dve_parts(before)[-1]), turn))
                        else:
                            pe.wait_ge(*act_side.after((before["id"], act_parts(before)[-1]), turn))
                        if PHASES[p][2]:
                            pe.wait_ge(wo_in, turn * 64 + 16 * (BIGS.index(p) + 1))
                    pe.wait_ge(*o_kept.after(groups[half - 1], turn))
                    w = wo_ring if PHASES[p][2] else wo[p]
                    for t in range(NT):
                        o = ps_x[q["aux"] % 2][:, t * D:(t + 1) * D]
                        for g in range(half - len(groups) // 2, half):
                            last = pe.matmul(o, ot[:, g, t * P:(t + 1) * P], w[:, g, :],
                                             start=(g == 0 and t == 0), stop=False)
                        if part == 1:
                            last = bias_row(o, f"yo{p}", stop=(t == NT - 1))
                    return last

                def piece(q):
                    kind, s = q["kind"], q["s"]
                    if kind not in AUX_KINDS:
                        return
                    if kind != "y":
                        await_inputs(q)
                    bank = ps_x[q["aux"] % 2]
                    if kind == "y":
                        last = out_projection(q, 1)
                    elif kind == "h":
                        src = x[s] if q["ln"] is None else xn
                        for t in range(NT):
                            last = pe.transpose(bank[:, t * P:(t + 1) * P], src[:, t, :], ident[:, :])
                    elif kind == "ff":
                        l, j = q["layer"], q["j"]
                        blocks = (j, j + 4) if l in (0, 2) else (2 * j, 2 * j + 1)
                        for k, c in enumerate(blocks):
                            last = three(bank[:, k * S:(k + 1) * S], w_up[l][:, 0, c * P:(c + 1) * P],
                                         w_up[l][:, 1, c * P:(c + 1) * P], ht[s][:, 0, :], ht[s][:, 1, :])
                    elif kind == "f":
                        l = q["layer"]
                        for t in range(NT):
                            o = bank[:, t * D:(t + 1) * D]
                            for j in range(FF // P):
                                pe.matmul(o, ft[:, j, t * P:(t + 1) * P], w_down[l][:, j, :], start=(j == 0), stop=False)
                            last = bias_row(o, f"fo{l}")
                    elif kind in ("q", "k"):
                        src, r = source(q)
                        p, j = q["p"], q["j"]
                        w = (wq if kind == "q" else wk)[p]
                        for k in range(2):
                            g = 2 * j + k
                            o = bank[:, k * S:(k + 1) * S]
                            masked = kind == "k" and PHASES[p][0] == 1
                            last = three(o, w[0:r, 0, g * P:(g + 1) * P], w[0:r, 1, g * P:(g + 1) * P],
                                         src[0:r, 0, :], src[0:r, 1, :], stop=not masked)
                            if masked:
                                last = pe.matmul(o, mask_rows[:, :], mask[s][:, p - 2, :], start=False, stop=True)
                    elif kind == "v":
                        src, r = source(q)
                        p, j = q["p"], q["j"]
                        if PHASES[p][2]:
                            i = BIGS.index(p)
                            pe.wait_ge(wv_in, turn * 64 + 16 * (i + 1))
                            t, half = j // 2, j % 2
                            w_hi = wv_ring[0:r, 0, half * 512:(half + 1) * 512]
                            w_lo = wv_ring[0:r, 1, half * 512:(half + 1) * 512]
                        else:
                            t = j
                            w_hi, w_lo = wv[p][0:r, 0, :], wv[p][0:r, 1, :]
                        last = three(bank[:, :], src[0:r, 0, t * P:(t + 1) * P], src[0:r, 1, t * P:(t + 1) * P],
                                     w_hi, w_lo, stop=PHASES[p][2])
                        if not PHASES[p][2]:
                            o = bank[:, :].rearrange("p (h e) -> p h e", e=32)[:, :, 0:DS]
                            i = ROWS[f"vb{p}"]
                            rr = 32 * (i % 4)
                            last = pe.matmul(o, ones[rr:rr + 1, :], rows[rr:rr + 1, i // 4, :].rearrange("p (h e) -> p h e", e=DS),
                                             start=False, stop=True)
                    last.then_inc(aux_ready.sem, 1)

                def make_t(n):
                    p, s, h = head(n)
                    if not PHASES[p][2]:
                        return
                    i = BIGS.index(p)
                    if h == 0:
                        pe.wait_ge(*dve_side.after((find("v", p=p, s=s, j=0)["h"]["id"], "lo"), turn))
                        if s == 0:
                            pe.wait_ge(g_in[i % 2], turn * 32 + 16 * (i // 2 + 1))
                    if n - 1 in tlo_ready.at:
                        pe.wait_ge(*tlo_ready.after(n - 1, turn))
                    elif BIG_HEADS.index(n) > 0:
                        pe.wait_ge(*tlo_ready.after(BIG_HEADS[BIG_HEADS.index(n) - 1], turn))
                    r = rows_of(p)
                    g = g_ring[i % 2]
                    three(ps_t[0:r, 0:S], g[:, 0, h, 0:r], g[:, 1, h, 0:r], ht[s][:, 0, :],
                          ht[s][:, 1, :]).then_inc(t_ready.sem, 1)

                def scores(n):
                    p, s, h = head(n)
                    bank = ps_s[n % 2]
                    if n >= 2:
                        pe.wait_ge(*exp_ready.after(n - 2, turn))
                    causal_phase = PHASES[p][0] == 1 and PHASES[p][1]
                    if PHASES[p][2]:
                        pe.wait_ge(*tlo_ready.after(n, turn))
                        if h == 0 and not PHASES[p][1]:
                            pe.wait_ge(*dve_side.after((find("in", s=s)["id"], "clo"), turn))
                        r = rows_of(p)
                        src = ht[s] if PHASES[p][1] else ct[s]
                        for t in range(NT):
                            last = three(bank[:, t, :], th[n % 2][0:r, 0, t * P:(t + 1) * P],
                                         th[n % 2][0:r, 1, t * P:(t + 1) * P], src[0:r, 0, :], src[0:r, 1, :])
                    else:
                        if h % 8 == 0:
                            pe.wait_ge(*dve_side.after((find("k", p=p, s=s, j=h // 8)["id"], "1"), turn))
                        g, r = h // 4, 32 * (h % 4)
                        for t in range(NT):
                            w = P * (t + 1) if causal_phase else S
                            last = pe.matmul(bank[:, t, 0:w], qs[s][r:r + 32, g, t * P:(t + 1) * P],
                                             ks[s][r:r + 32, g, 0:w], start=True, stop=not causal_phase)
                            if causal_phase:
                                last = pe.matmul(bank[:, t, t * P:(t + 1) * P], ident_bf[:, :], causal[:, :],
                                                 start=False, stop=True)
                    last.then_inc(s_ready.sem, 1)

                def turn_p(n):
                    p, s, h = head(n)
                    pe.wait_ge(*pn_ready.after(n, turn))
                    if n >= 1:
                        pe.wait_ge(*pt_ready.after(n - 1, turn))
                    causal_phase = PHASES[p][0] == 1 and PHASES[p][1]
                    if causal_phase:
                        blocks = [(0, 0, 0), (0, 1, P), (1, 1, 2 * P)]
                    else:
                        blocks = [(k, t, k * S + t * P) for k in range(NT) for t in range(NT)]
                    for k, t, at in blocks:
                        last = pe.transpose(ps_p[:, at:at + P], pn[n % 3][:, t, k * P:(k + 1) * P], ident[:, :])
                    last.then_inc(tr_ready.sem, 1)

                def output(n):
                    p, s, h = head(n)
                    g = GROUPS.index(group_of(n))
                    pe.wait_ge(*pt_ready.after(n, turn))
                    if h == 0:
                        q = find("v", p=p, s=s, j=3 if PHASES[p][2] else 1)
                        pe.wait_ge(*act_side.after((q["id"], "v"), turn))
                    if g >= 2 and (n == 0 or group_of(n - 1) != group_of(n)):
                        pe.wait_ge(*o_kept.after(GROUPS[g - 2], turn))
                    bank = ps_o[g % 2]
                    causal_phase = PHASES[p][0] == 1 and PHASES[p][1]
                    for k in range(NT):
                        if PHASES[p][2]:
                            r, m = 64 * (h % 2), 64
                            w = v[s][:, k * INNER + h * DH:k * INNER + (h + 1) * DH]
                        else:
                            r, m = 32 * (h % 4), 32
                            w = v[s][:, k * 512 + h * 32:k * 512 + (h + 1) * 32]
                        if causal_phase and k == 1:
                            o, mov = bank[r:r + m, P:S], pt[n % 2][:, 2 * P:3 * P]
                        else:
                            o, mov = bank[r:r + m, 0:S], pt[n % 2][:, k * S:(k + 1) * S]
                        last = pe.matmul(o, w, mov, start=(k == 0), stop=(k == NT - 1))
                    last.then_inc(o_ready.sem, 1)

                for i in range(FIRST_STEP, LAST_STEP + 1):
                    if 0 <= i - 4 < HEAD_N:
                        turn_p(i - 4)
                    if 0 <= i - 1 < HEAD_N:
                        scores(i - 1)
                    if 0 <= i - 5 < HEAD_N:
                        output(i - 5)
                    if 0 <= i + 1 < HEAD_N:
                        make_t(i + 1)
                    for q in STEPS.get(i, []):
                        piece(q)
                    for q in STEPS.get(i + 1, []):
                        if q["kind"] == "y":
                            out_projection(q, 0)

        @block.scalar
        def _(act):
            for j, job in enumerate(jobs):
                if job["kind"] == "g":
                    r = rows_of(BIGS[job["i"]])
                    ring = g_ring[job["i"] % 2]
                    if job["i"] < 2:
                        act.wait_ge(g_out[job["i"] + 2], 16)
                    for k in range(4):
                        n = banks_of[j][k]
                        half, par = k // 2, k % 2
                        act.wait_ge(g_made, n + 1)
                        src = (setup_banks[n % 4][:, :, :].rearrange("p a b -> p (a b)") if n % 4 < 2
                               else setup_banks[n % 4][:, :]).rearrange("p (t c) -> p t c", c=P)[:, :, 0:r]
                        dst = ring[:, 0, 8 * half + par:8 * half + par + 7:2, 0:r]
                        act.activation(dst, src, ACT.Copy, scale=BIG_SCALE).then_inc(g_hi, 1)
                else:
                    u = job["areas"][0]
                    r, n = job["src"][0].shape
                    act.wait_ge(raw_in[u % NA], 16 * (u // NA + 1))
                    if job["store"] == 1:
                        act.wait_ge(wv_out[2], 32)
                    act.activation(job["hi"][0:r, :], raw(u, r, n), ACT.Copy, scale=job["scale"]).then_inc(split_hi, 1)

            with act.Fori(0, TURNS) as turn:

                def piece(q):
                    kind, s = q["kind"], q["s"]
                    if kind == "in":
                        act.wait_ge(xin[s], turn * 48 + 48)
                        act.activation(ct[s][:, 0, :], c_in[s][:, :], ACT.Copy).then_inc(act_side.sem, 1)
                    if kind not in AUX_KINDS or not act_parts(q):
                        return
                    act.wait_ge(*aux_ready.after(q["id"], turn))
                    bank, tmp = ps_x[q["aux"] % 2], side[q["aux"] % 2]
                    if kind == "h":
                        if q["ln"] is None:
                            act.activation(tmp[:, 0:S], bank[:, 0:S], ACT.Copy).then_inc(act_side.sem, 1)
                        else:
                            act.activation(tmp[:, 0:S], bank[:, 0:S], ACT.Identity, bias=col(f"b{q['ln']}"),
                                           scale=col(f"g{q['ln']}")).then_inc(act_side.sem, 1)
                    elif kind == "ff":
                        l, j = q["layer"], q["j"]
                        if l in (0, 2):
                            act.activation(tmp[:, 0:S], bank[:, S:2 * S], ACT.Gelu,
                                           bias=col(f"ffb{l}_{4 + j}")).then_inc(act_side.sem, 1)
                        else:
                            for k in range(2):
                                act.activation(ft[:, 2 * j + k, :], bank[:, k * S:(k + 1) * S], ACT.Gelu,
                                               bias=col(f"ffb{l}_{2 * j + k}")).then_inc(act_side.sem, 1)
                    elif kind in ("q", "k"):
                        for k in range(2):
                            name = f"{kind}mb{q['p']}_{2 * q['j'] + k}"
                            act.activation(tmp[:, k * S:(k + 1) * S].bitcast(F32R), bank[:, k * S:(k + 1) * S],
                                           ACT.Identity, bias=col(name), scale=col("m" + kind)).then_inc(act_side.sem, 1)
                    elif kind == "v":
                        p, j = q["p"], q["j"]
                        act.activation(v[s][:, j * 512:(j + 1) * 512], bank[:, :], ACT.Copy).then_inc(act_side.sem, 1)

                def exps(n):
                    p, s, h = head(n)
                    act.wait_ge(*max_ready.after(n, turn))
                    if n >= 2:
                        act.wait_ge(*pn_ready.after(n - 2, turn))
                    causal_phase = PHASES[p][0] == 1 and PHASES[p][1]
                    for t in range(NT):
                        w = P * (t + 1) if causal_phase else S
                        last = act.activation(pr[n % 2][:, t, 0:w], ps_s[n % 2][:, t, 0:w], ACT.Exp,
                                              bias=negmax[:, n % 4, t:t + 1], accum_out=den[:, n % 4, t:t + 1])
                    last.then_inc(exp_ready.sem, 1)

                def t_high(n):
                    p = head(n)[0]
                    if not PHASES[p][2]:
                        return
                    r = rows_of(p)
                    act.wait_ge(*t_ready.after(n, turn))
                    act.activation(th[n % 2][0:r, 0, :], ps_t[0:r, 0:S], ACT.Copy).then_inc(thi_ready.sem, 1)

                def keep_output(n):
                    if GROUP_LAST[group_of(n)] != n:
                        return
                    act.wait_ge(*o_ready.after(n, turn))
                    g = group_of(n)
                    act.activation(ot[:, g[2], :], ps_o[GROUPS.index(g) % 2][:, 0:S], ACT.Copy).then_inc(o_kept.sem, 1)

                for i in range(FIRST_STEP, LAST_STEP + 1):
                    if 0 <= i < HEAD_N:
                        t_high(i)
                    for q in STEPS.get(i - 1, []):
                        piece(q)
                    if 0 <= i - 2 < HEAD_N:
                        exps(i - 2)
                    if 0 <= i - 6 < HEAD_N:
                        keep_output(i - 6)

        @block.vector
        def _(dve):
            count = [0]

            def const(ins):
                count[0] += 1
                ins.then_inc(const_done, 1)

            dve.wait_ge(const_in, 16 * SETUP_CONSTS)
            const(dve.tensor_copy(ident_bf[:, :], ident[:, :]))
            const(dve.tensor_copy(causal[:, :], xn[:, 0, :]))
            const(dve.tensor_copy(mask_rows[:, :], xn[0:1, 1, :]))
            q0, q1 = COLS[f"qb{SMALLS[0]}_0"], COLS["mq"]
            tmp = side[0][:, 0:q1 - q0]
            const(dve.tensor_tensor(tmp, cols[:, q0:q1], pr[0][:, 0, 0:q1 - q0], ALU.mult))
            dve.wait_ge(const_done, 4)
            const(dve.tensor_tensor(cols[:, q0:q1], tmp, pr[0][:, 1, 0:q1 - q0], ALU.add))
            assert count[0] == CONST_OPS
            for j, job in enumerate(jobs):
                if job["kind"] == "g":
                    r = rows_of(BIGS[job["i"]])
                    ring = g_ring[job["i"] % 2]
                    for k in range(4):
                        n = banks_of[j][k]
                        half, par = k // 2, k % 2
                        dve.wait_ge(g_hi, n + 1)
                        src = (setup_banks[n % 4][:, :, :].rearrange("p a b -> p (a b)") if n % 4 < 2
                               else setup_banks[n % 4][:, :]).rearrange("p (t c) -> p t c", c=P)[:, :, 0:r]
                        h0 = 8 * half + par
                        dve.scalar_tensor_tensor(out=ring[:, 1, h0:h0 + 7:2, 0:r], in0=src, scalar=BIG_SCALE,
                                                 in1=f32(ring[:, 0, h0:h0 + 7:2, 0:r]), op0=ALU.mult,
                                                 op1=ALU.subtract).then_inc(g_lo, 1)
                else:
                    u = job["areas"][0]
                    r, n = job["src"][0].shape
                    dve.wait_ge(split_hi, job["n"] + 1)
                    dve.scalar_tensor_tensor(out=job["lo"][0:r, :], in0=raw(u, r, n), scalar=job["scale"],
                                             in1=f32(job["hi"][0:r, :]), op0=ALU.mult,
                                             op1=ALU.subtract).then_inc(raw_used, 1)

            with dve.Fori(0, TURNS) as turn:

                def tick(ins):
                    ins.then_inc(dve_side.sem, 1)

                def norm_stats(q, src):
                    for t in range(NT):
                        tick(dve.bn_stats(stats[:, t, :], src[:, t, :]))
                    dve.wait_ge(*dve_side.after((q["id"], "st1"), turn))
                    dve.memset(fence[:, :], 0.0)
                    for t in range(NT):
                        tick(dve.bn_aggr(mv[:, t, :], stats[:, t, :]))
                    dve.wait_ge(*dve_side.after((q["id"], "mv1"), turn))
                    tick(dve.tensor_scalar(ve[:, :], mv[:, :, 1], EPS, None, ALU.add))

                def piece(q):
                    kind, s = q["kind"], q["s"]
                    if kind == "in":
                        dve.wait_ge(xin[s], turn * 48 + 48)
                        dve.wait_ge(out_done, turn * 32 + 16)
                        tick(dve.tensor_copy(x[s][:, :, :], x_in[s][:, :, :]))
                        dve.wait_ge(*act_side.after((q["id"], "chi"), turn))
                        tick(dve.tensor_tensor(ct[s][:, 1, :], c_in[s][:, :], f32(ct[s][:, 0, :]), ALU.subtract))
                        tick(dve.tensor_scalar(mask[s][:, :, :], m_in[s][:, :, :], BIG, None, ALU.mult))
                        dve.wait_ge(*dve_side.after((q["id"], "mask"), turn))
                        norm_stats(q, x[s])
                        dve.wait_ge(*dve_side.after((q["id"], "ve"), turn))
                        dve.sem_inc(x_taken, 1)
                    elif kind == "y":
                        p = q["p"]
                        bank = ps_x[q["aux"] % 2][:, 0:S].rearrange("p (t d) -> p t d", d=D)
                        dve.wait_ge(*aux_ready.after(q["id"], turn))
                        if p == 6:
                            tick(dve.tensor_copy(x3[:, :, :], bank))
                        else:
                            tick(dve.tensor_tensor(x[s][:, :, :], bank, x[s][:, :, :], ALU.add))
                        dve.wait_ge(*dve_side.after((q["id"], "x"), turn))
                        norm_stats(q, x3 if p == 6 else x[s])
                    elif kind == "f":
                        bank = ps_x[q["aux"] % 2][:, 0:S].rearrange("p (t d) -> p t d", d=D)
                        dve.wait_ge(*aux_ready.after(q["id"], turn))
                        tick(dve.tensor_tensor(x[s][:, :, :], bank, x[s][:, :, :], ALU.add))
                        if "ve" in dve_parts(q):
                            dve.wait_ge(*dve_side.after((q["id"], "x"), turn))
                            norm_stats(q, x[s])
                    elif kind == "xn":
                        before = [o for o in ORDER[:ORDER.index(q)] if o["s"] == s and "ve" in dve_parts(o)][-1]
                        dve.wait_ge(*rstd_ready.after(before["id"], turn))
                        src = x3 if q["p"] == 6 else x[s]
                        for t in range(NT):
                            tick(dve.tensor_scalar(xn[:, t, :], src[:, t, :], mv[:, t, 0:1], rstd[:, t:t + 1],
                                                   ALU.subtract, ALU.mult))
                        if q["p"] == 6:
                            tick(dve.tensor_tensor(x[s][:, :, :], x[s][:, :, :], x3[:, :, :], ALU.add))
                    elif kind == "h":
                        tmp = side[q["aux"] % 2]
                        dve.wait_ge(*act_side.after((q["id"], "h"), turn))
                        tick(dve.tensor_copy(ht[s][:, 0, :], tmp[:, 0:S]))
                        dve.wait_ge(*dve_side.after((q["id"], "hi"), turn))
                        tick(dve.tensor_tensor(ht[s][:, 1, :], tmp[:, 0:S], f32(ht[s][:, 0, :]), ALU.subtract))
                    elif kind == "ff" and dve_parts(q):
                        l, j = q["layer"], q["j"]
                        dve.wait_ge(*act_side.after((q["id"], "ff"), turn))
                        tick(dve.scalar_tensor_tensor(out=ft[:, j, :], in0=ps_x[q["aux"] % 2][:, 0:S],
                                                      scalar=col(f"ffb{l}_{j}"), in1=side[q["aux"] % 2][:, 0:S],
                                                      op0=ALU.add, op1=ALU.mult))
                    elif kind in ("q", "k"):
                        dst = (qs if kind == "q" else ks)[s]
                        dve.wait_ge(*act_side.after((q["id"], "1"), turn))
                        for k in range(2):
                            g = 2 * q["j"] + k
                            tick(dve.scalar_tensor_tensor(out=dst[:, g, :], in0=ps_x[q["aux"] % 2][:, k * S:(k + 1) * S],
                                                          scalar=col(f"{kind}b{q['p']}_{g}"),
                                                          in1=side[q["aux"] % 2][:, k * S:(k + 1) * S],
                                                          op0=ALU.add, op1=ALU.subtract))

                def t_low(n):
                    p = head(n)[0]
                    if not PHASES[p][2]:
                        return
                    r = rows_of(p)
                    dve.wait_ge(*thi_ready.after(n, turn))
                    dve.tensor_tensor(th[n % 2][0:r, 1, :], ps_t[0:r, 0:S], f32(th[n % 2][0:r, 0, :]),
                                      ALU.subtract).then_inc(tlo_ready.sem, 1)

                def row_max(n):
                    p = head(n)[0]
                    dve.wait_ge(*s_ready.after(n, turn))
                    bank = ps_s[n % 2]
                    if PHASES[p][0] != 1:
                        dve.tensor_reduce(negmax[:, n % 4, :], bank[:, :, :], AX.X, ALU.max,
                                          negate=True).then_inc(max_ready.sem, 1)
                        return
                    if PHASES[p][1]:
                        dve.tensor_reduce(raw_negmax[:, n % 4, 0:1], bank[:, 0, 0:P], AX.X, ALU.max, negate=True)
                        dve.tensor_reduce(raw_negmax[:, n % 4, 1:2], bank[:, 1, :], AX.X, ALU.max,
                                          negate=True).then_inc(raw_max.sem, 1)
                    else:
                        dve.tensor_reduce(raw_negmax[:, n % 4, :], bank[:, :, :], AX.X, ALU.max,
                                          negate=True).then_inc(raw_max.sem, 1)
                    dve.wait_ge(*raw_max.after(n, turn))
                    dve.tensor_scalar(negmax[:, n % 4, :], raw_negmax[:, n % 4, :], 8.0, 0.125, ALU.mult,
                                      ALU.mult).then_inc(max_ready.sem, 1)

                def over_sum(n):
                    dve.wait_ge(*exp_ready.after(n, turn))
                    dve.reciprocal(rden[:, n % 4, :], den[:, n % 4, :]).then_inc(rden_ready.sem, 1)

                def keep_pt(n):
                    p = head(n)[0]
                    dve.wait_ge(*tr_ready.after(n, turn))
                    w = 3 * P if PHASES[p][0] == 1 and PHASES[p][1] else NT * S
                    dve.tensor_copy(pt[n % 2][:, 0:w], ps_p[:, 0:w]).then_inc(pt_ready.sem, 1)

                for i in range(FIRST_STEP, LAST_STEP + 1):
                    if 0 <= i < HEAD_N:
                        t_low(i)
                    if 0 <= i - 4 < HEAD_N:
                        keep_pt(i - 4)
                    for q in STEPS.get(i - 1, []):
                        piece(q)
                    if 0 <= i - 1 < HEAD_N:
                        row_max(i - 1)
                    if 0 <= i - 2 < HEAD_N:
                        over_sum(i - 2)

        @block.gpsimd
        def _(pool):
            pool.wait_ge(const_in, 16 * SETUP_CONSTS)
            neghalf = cols[:, COLS["neghalf0"]:COLS["neghalf0"] + NT]
            with pool.Fori(0, TURNS) as turn:

                def normalise(n):
                    p = head(n)[0]
                    pool.wait_ge(*rden_ready.after(n, turn))
                    if n >= 3:
                        pool.wait_ge(*tr_ready.after(n - 3, turn))
                    if PHASES[p][0] == 1 and PHASES[p][1]:
                        for t in range(NT):
                            w = P * (t + 1)
                            last = pool.tensor_tensor(pn[n % 3][:, t, 0:w], pr[n % 2][:, t, 0:w],
                                                      rden[:, n % 4, t:t + 1].to_broadcast([P, w]), ALU.mult)
                    else:
                        last = pool.tensor_tensor(pn[n % 3][:, :, :], pr[n % 2][:, :, :],
                                                  rden[:, n % 4, :].unsqueeze(2).to_broadcast([P, NT, S]), ALU.mult)
                    last.then_inc(pn_ready.sem, 1)

                def piece(q):
                    if "ve" in dve_parts(q):
                        pool.wait_ge(*dve_side.after((q["id"], "ve"), turn))
                        pool.tensor_tensor(rstd[:, :], ve[:, :], neghalf, ALU.pow).then_inc(rstd_ready.sem, 1)

                for i in range(FIRST_STEP, LAST_STEP + 1):
                    if 0 <= i - 2 < HEAD_N:
                        normalise(i - 2)
                    for q in STEPS.get(i - 1, []):
                        piece(q)


def stacked(w, order):
    r = w.shape[0]
    o = np.zeros((r, HEADS, 32), w.dtype)
    for at in order:
        o[:, :, at:at + DS] = w.reshape(r, HEADS, DS)
    return np.ascontiguousarray(o.reshape(r, HEADS * 32))


def layout(i):
    f = {k: np.asarray(w) for k, w in i.items()}
    a = {}
    a["x"] = np.ascontiguousarray(f["x"].reshape(B, NT, P, D).transpose(0, 2, 1, 3))
    a["c"] = np.ascontiguousarray(f["ctx_768"].transpose(0, 2, 1))
    a["m"] = np.ascontiguousarray(np.stack([f["mask_BxS_bf0"], f["mask_BxS2_bf0"]], 1))
    L0, L1, L2, L3 = (f"L{k}_xattn_" for k in range(4))
    big = [(L0 + "Wq1", L0 + "Wk1", L0 + "Wv1", L0 + "Wo1"), (L0 + "Wq2", L0 + "Wk2", L0 + "Wv2", L0 + "Wo2"),
           (L2 + "a1_wq", L2 + "a1_wk", L2 + "a1_wv", L2 + "a1_wo"),
           (L2 + "a2_wq", L2 + "a2_wk", L2 + "a2_wv", L2 + "a2_wo")]
    for n, (q, k, vv, o) in enumerate(big):
        for nm, w in (("wqt", f[q]), ("wkt", f[k])):
            t = w.T.reshape(HEADS // 2, P, w.shape[0]).transpose(1, 0, 2)
            a[f"{nm}{n}"] = np.ascontiguousarray(t.reshape(P, -1))
        a[f"wv{n}"] = np.ascontiguousarray(f[vv])
        a[f"wo{n}"] = np.ascontiguousarray(f[o].reshape(HEADS // 2, P, D).transpose(1, 0, 2))
    qkv, qkvb = f[L1 + "qkv_w"], f[L1 + "qkv_b"]
    small = {2: (qkv[:, 0:D], qkv[:, D:2 * D], qkv[:, 2 * D:], f[L1 + "proj_w"], qkvb[0:D], qkvb[D:2 * D], qkvb[2 * D:]),
             3: (f[L1 + "q_w"], f[L1 + "k_w"], f[L1 + "v_w"], f[L1 + "out_w"], f[L1 + "q_b"], f[L1 + "k_b"], f[L1 + "v_b"]),
             6: (f[L3 + "Wq"], f[L3 + "Wk"], f[L3 + "Wv"], f[L3 + "Wo"], f[L3 + "bq"], f[L3 + "bk"], f[L3 + "bv"])}
    Q_ALL, K_ALL, Q_LO, K_LO = (0, 8, 16), (0, 8, 16), (16,), (8,)
    cols = np.zeros((P, len(COLS)), np.float32)
    rows = np.zeros((P, ROW_W, D), np.float32)

    def put_row(name, w):
        rows[32 * (ROWS[name] % 4), ROWS[name] // 4, :] = w

    for p, (q, k, vv, o, bq, bk, bv) in small.items():
        a[f"wq{p}s"], a[f"wk{p}s"], a[f"wv{p}s"] = stacked(q, Q_ALL), stacked(k, K_ALL), stacked(vv, (0,))
        oo = np.zeros((QUADS, 4, 32, D), np.float32)
        oo[:, :, 0:DS] = o.reshape(QUADS, 4, DS, D)
        a[f"wo{p}s"] = np.ascontiguousarray(oo.reshape(QUADS, P, D).transpose(1, 0, 2))
        for kind, w, places in (("qb", bq, Q_ALL), ("qmb", bq, Q_LO), ("kb", bk, K_ALL), ("kmb", bk, K_LO)):
            t = stacked(w.reshape(1, -1), places).reshape(QUADS, P)
            for g in range(QUADS):
                cols[:, COLS[f"{kind}{p}_{g}"]] = t[g]
        put_row(f"vb{p}", bv)
    lns = [L0 + "g1", L0 + "g2", L0 + "g3", L1 + "ln1_w", L1 + "ln2_w", L1 + "ln3_w",
           L2 + "ln1_g", L2 + "ln2_g", L2 + "ln3_g", L3 + "ln_g"]
    lnb = [L0 + "b1", L0 + "b2", L0 + "b3", L1 + "ln1_b", L1 + "ln2_b", L1 + "ln3_b",
           L2 + "ln1_b", L2 + "ln2_b", L2 + "ln3_b", L3 + "ln_b"]
    for n in range(10):
        cols[:, COLS[f"g{n}"]] = f[lns[n]]
        cols[:, COLS[f"b{n}"]] = f[lnb[n]]
    ff = [(L0 + "Wp", L0 + "bp", L0 + "Wf", L0 + "bf"), (L1 + "mlp1_w", L1 + "mlp1_b", L1 + "mlp2_w", L1 + "mlp2_b"),
          (L2 + "ff_w1", L2 + "ff_b1", L2 + "ff_w2", L2 + "ff_b2"), (L3 + "W1", L3 + "b1", L3 + "W2", L3 + "b2")]
    for l, (w1, b1, w2, b2) in enumerate(ff):
        a[f"w_up{l}"] = np.ascontiguousarray(f[w1])
        a[f"w_down{l}"] = np.ascontiguousarray(f[w2].reshape(FF // P, P, D).transpose(1, 0, 2))
        for j in range(f[b1].shape[0] // P):
            cols[:, COLS[f"ffb{l}_{j}"]] = f[b1][j * P:(j + 1) * P]
        put_row(f"fo{l}", f[b2])
    outs = [L0 + "bo1", L0 + "bo2", L1 + "proj_b", L1 + "out_b", L2 + "a1_bo", L2 + "a2_bo", L3 + "bo"]
    for p, nm in enumerate(outs):
        put_row(f"yo{p}", f[nm])
    r32 = np.arange(P) % 32
    cols[:, COLS["mq"]] = (r32 >= 16) & (r32 < 24)
    cols[:, COLS["mk"]] = (r32 >= 8) & (r32 < 16)
    cols[:, COLS["neghalf0"]] = cols[:, COLS["neghalf1"]] = -0.5
    a["cols"], a["rows"] = cols, rows
    a["ident"], a["ones"] = np.eye(P, dtype=np.float32), np.ones((P, P), np.float32)
    masks = np.zeros((P, NT, D), np.float32)
    masks[:, 0, :] = np.where(np.arange(P)[None, :] > np.arange(P)[:, None], np.float32(BIG), np.float32(0))
    masks[0, 1, :] = r32 == 24
    a["masks"] = masks
    fix = np.zeros((P, NT, S), np.float32)
    q0, q1 = COLS[f"qb{SMALLS[0]}_0"], COLS["mq"]
    for name, c in COLS.items():
        if q0 <= c < q1:
            fix[:, 0, c - q0] = np.float32(SMALL_SCALE) if name[0] == "q" else 1.0
            if name.startswith(("qb2", "qb3")):
                fix[:, 1, c - q0] = r32 == 24
    a["bias_ones"] = np.ascontiguousarray(fix.reshape(P, NT * S))
    return a


def kernel(**inputs):
    import concourse.bacc as bacc
    from concourse.bass_utils import run_bass_kernel_spmd

    arrays = {f"in_{k}": w for k, w in layout(inputs).items()}
    nc = bacc.Bacc("TRN2", target_bir_lowering=False, num_devices=1)
    aps = {k[3:]: nc.dram_tensor(k, w.shape, mybir.dt.from_np(w.dtype), kind="ExternalInput").ap()
           for k, w in arrays.items()}
    out = nc.dram_tensor("out_0", (B, P, NT, D), F32, kind="ExternalOutput").ap()
    build(nc, aps, out)
    r = run_bass_kernel_spmd(nc, [arrays], core_ids=[0])
    y = r.results[0]["out_0"]
    return np.ascontiguousarray(y.transpose(0, 2, 1, 3)).reshape(B, S, D)
```

```python
from contextlib import ExitStack

import numpy as np

import concourse.bass as bass
from concourse import mybir

F32 = mybir.dt.float32
F32R = mybir.dt.float32r
BF16 = mybir.dt.bfloat16
U8 = mybir.dt.uint8
ALU = mybir.AluOpType
ACT = mybir.ActivationFunctionType
AX = mybir.AxisListType

B, S, D, C = 8, 256, 128, 96
HEADS, DH, DS = 16, 64, 8
INNER = HEADS * DH
FF = 512
P = 128
NT = S // P
SLOTS = 2
ROUNDS = 2
TURNS = B // SLOTS // ROUNDS
EPS = 1e-5
BIG = -1.0e38
SMALL_SCALE = float(DS) ** -0.5
BIG_SCALE = float(DH) ** -0.5

PHASES = [(0, True, True), (0, False, True), (1, True, False), (1, False, False),
          (2, True, True), (2, False, True), (3, False, False)]
NP = len(PHASES)
BIGS = [p for p, ph in enumerate(PHASES) if ph[2]]
SMALLS = [p for p, ph in enumerate(PHASES) if not ph[2]]
PHASES = PHASES * ROUNDS
QUADS = HEADS // 4
LAYERS = 4


def rows_of(p):
    return D if PHASES[p][1] else C


def column_names():
    names = []
    for ln in range(10):
        names += [f"g{ln}", f"b{ln}"]
    for layer in range(LAYERS):
        names += [f"ffb{layer}_{j}" for j in range(8 if layer in (0, 2) else 4)]
    for p in SMALLS:
        for kind in ("qb", "qmb", "kb", "kmb"):
            names += [f"{kind}{p}_{g}" for g in range(QUADS)]
    names += ["mq", "mk", "neghalf0", "neghalf1"]
    return names


def row_names():
    return [f"yo{p}" for p in range(NP)] + [f"fo{l}" for l in range(LAYERS)] + [f"vb{p}" for p in SMALLS]


COLS = {n: i for i, n in enumerate(column_names())}
ROWS = {n: i for i, n in enumerate(row_names())}
ROW_W = (len(ROWS) + 3) // 4


class Tally:

    def __init__(self, sem, keys):
        self.sem, self.at, self.total = sem, {k: i + 1 for i, k in enumerate(keys)}, len(keys)
        assert len(self.at) == self.total

    def after(self, key, turn):
        return self.sem, turn * self.total + self.at[key]

    def last(self, keys):
        return max(keys, key=self.at.get)


Y_PARTS = 4
FF_PACE = {1: (1, 2, 1, 1), 3: (2, 2, 1, 1), 5: (2, 2, 1, 1), 6: (1, 2, 1, 1)}
HEAD_N = len(PHASES) * SLOTS * HEADS


def head(n):
    return n // (SLOTS * HEADS), n // HEADS % SLOTS, n % HEADS


def big_number(p):
    return p // NP * len(BIGS) + BIGS.index(p % NP)


def first_head(p, s):
    return (p * SLOTS + s) * HEADS


LN_BEFORE = {0: 0, 1: 1, 2: 3, 3: 4, 4: 6, 5: 7}
LN_FF = {0: 2, 1: 5, 2: 8, 3: 9}


def plan():
    steps = {}
    pieces = []

    def put(step, kind, **kw):
        piece = dict(kind=kind, id=len(pieces), step=step, **kw)
        pieces.append(piece)
        steps.setdefault(step, []).append(piece)
        return piece

    def inputs_of(p, s, at, h):
        if PHASES[p][2]:
            order = [("v", j) for j in range(4)]
        else:
            order = [("q", 0), ("k", 0), ("v", 0), ("v", 1), ("q", 1), ("k", 1)]
        for kind, j in order:
            put(at, kind, p=p, s=s, j=j, h=h)
            at += 1

    def after_phase(p, s, at):
        layer = PHASES[p][0]
        put(at, "y", p=p, s=s)
        x = put(at + 1, "xn", p=p, s=s, of="y")
        if p % NP + 1 < NP and PHASES[p + 1][0] == layer:
            h = put(at + 3, "h", s=s, ln=LN_BEFORE[(p + 1) % NP], x=x)
            inputs_of(p + 1, s, at + 4, h)
            return
        to_h, a_step, to_f, to_next = FF_PACE[p % NP]
        at += 1 + to_h
        h = put(at, "h", s=s, ln=LN_FF[layer], x=x)
        n = 4 if layer in (0, 2) else 2
        ffs = [put(at + 1 + j // a_step, "ff", p=p, s=s, layer=layer, j=j, h=h) for j in range(n)]
        at = ffs[-1]["step"] + to_f
        f = put(at, "f", p=p, s=s, layer=layer, ffs=ffs)
        if p + 1 == len(PHASES):
            return
        if p % NP + 1 == NP:
            start(p + 1, s, at + to_next)
            return
        if p % NP + 1 in LN_BEFORE:
            x = put(at + 1, "xn", p=p, s=s, of="f")
            h = put(at + 1 + to_next, "h", s=s, ln=LN_BEFORE[p % NP + 1], x=x)
        else:
            h = put(at + to_next, "h", s=s, ln=None, x=f)
        inputs_of(p + 1, s, h["step"] + 1, h)

    def start(p, s, at):
        put(at, "in", p=p, s=s)
        x = put(at + 1, "xn", p=p, s=s, of="in")
        h = put(at + 2, "h", s=s, ln=LN_BEFORE[0], x=x)
        inputs_of(p, s, at + 3, h)

    start(0, 0, -4)
    start(0, 1, 4)
    for p in range(len(PHASES)):
        for s in range(SLOTS):
            after_phase(p, s, first_head(p, s) + HEADS + 6)
    order = [q for i in sorted(steps) for q in steps[i]]
    return steps, order


STEPS, ORDER = plan()
FIRST_STEP, LAST_STEP = min(STEPS), max(max(STEPS) + 1, HEAD_N + 7)
AUX_KINDS = ("y", "h", "ff", "f", "q", "k", "v")
AUX = [q for q in ORDER if q["kind"] in AUX_KINDS]
for _i, _q in enumerate(AUX):
    _q["aux"] = _i


def third_sum(q):
    return q["p"] % NP == NP - 1 and q.get("of", "y") == "y"


def dve_parts(q):
    k = q["kind"]
    if k == "in":
        return ["x", "clo", "mask"] + ["st0", "st1", "mv0", "mv1", "ve"]
    if k == "y":
        return ["x"] + ["st0", "st1", "mv0", "mv1", "ve"]
    if k == "f":
        if q["p"] % NP + 1 not in LN_BEFORE:
            return ["x"]
        return ["x"] + ["st0", "st1", "mv0", "mv1", "ve"]
    if k == "xn":
        return ["xn0", "xn1"] + (["res"] if third_sum(q) else [])
    if k == "h":
        return ["hi", "lo"]
    if k == "ff":
        return ["ff"] if q["layer"] in (0, 2) else []
    if k in "qk":
        return ["0", "1"]
    return []


def act_parts(q):
    k = q["kind"]
    if k == "in":
        return ["chi"]
    if k == "h":
        return ["h"]
    if k == "ff":
        return ["ff"] if q["layer"] in (0, 2) else ["ff0", "ff1"]
    if k in ("q", "k"):
        return ["0", "1"]
    if k == "v":
        return ["v"]
    return []


def group_of(n):
    p, s, h = head(n)
    return (p, s, h // (2 if PHASES[p][2] else 4))


GROUPS = list(dict.fromkeys(group_of(n) for n in range(HEAD_N)))
GROUP_LAST = {group_of(n): n for n in range(HEAD_N)}
BIG_HEADS = [n for n in range(HEAD_N) if PHASES[head(n)[0]][2]]


def find(kind, **kw):
    got = [q for q in ORDER if q["kind"] == kind and all(q.get(k) == v for k, v in kw.items())]
    assert len(got) == 1, (kind, kw, len(got))
    return got[0]


def build(nc, a, out):
    with ExitStack() as ctx:
        def sb(name, shape, dt=F32):
            return ctx.enter_context(nc.sbuf_tensor(name, shape, dt))

        def sem(name):
            return ctx.enter_context(nc.semaphore(name))

        g_ring = [sb(f"g_ring{i}", [P, 2, HEADS, P], F32R) for i in range(2)]
        wv_ring = sb("wv_ring", [P, 2, INNER], F32R)
        wo_ring = sb("wo_ring", [P, HEADS // 2, D])
        w_up = {l: sb(f"w_up{l}", [P, 2, 2 * FF if l in (0, 2) else FF], F32R) for l in range(LAYERS)}
        w_down = {l: sb(f"w_down{l}", [P, FF // P, D]) for l in range(LAYERS)}
        wq = {p: sb(f"wq{p}", [P, 2, QUADS * P], F32R) for p in SMALLS}
        wk = {p: sb(f"wk{p}", [P, 2, QUADS * P], F32R) for p in SMALLS}
        wv = {p: sb(f"wv{p}", [P, 2, QUADS * P], F32R) for p in SMALLS}
        wo = {p: sb(f"wo{p}", [P, QUADS, D]) for p in SMALLS}
        cols = sb("cols", [P, len(COLS)])
        rows = sb("rows", [P, ROW_W, D])
        ident = sb("ident", [P, P])
        ones = sb("ones", [P, P])
        ident_bf = sb("ident_bf", [P, P], BF16)
        causal = sb("causal", [P, P], BF16)
        mask_rows = sb("mask_rows", [1, P], BF16)

        x = [sb(f"x{s}", [P, NT, D]) for s in range(SLOTS)]
        x_in = [sb(f"x_in{s}", [P, NT, D]) for s in range(SLOTS)]
        c_in = [sb(f"c_in{s}", [C, S]) for s in range(SLOTS)]
        m_in = [sb(f"m_in{s}", [1, 2, S], U8) for s in range(SLOTS)]
        mask = [sb(f"mask{s}", [1, 2, S], BF16) for s in range(SLOTS)]
        ht = [sb(f"ht{s}", [P, 2, S], F32R) for s in range(SLOTS)]
        ct = [sb(f"ct{s}", [C, 2, S], F32R) for s in range(SLOTS)]
        v = [sb(f"v{s}", [P, NT * INNER]) for s in range(SLOTS)]
        qs = [sb(f"qs{s}", [P, QUADS, S], F32R) for s in range(SLOTS)]
        ks = [sb(f"ks{s}", [P, QUADS, S], F32R) for s in range(SLOTS)]
        ot = sb("ot", [P, HEADS // 2, S])
        xn = sb("xn", [P, NT, D])
        side = [sb(f"side{i}", [P, 2 * S]) for i in range(2)]
        ft = sb("ft", [P, FF // P, S])
        x3 = sb("x3", [P, NT, D])
        stats = sb("stats", [P, NT, 6])
        mv = sb("mv", [P, NT, 2])
        ve = sb("ve", [P, NT])
        fence = sb("fence", [P, 1])
        rstd = sb("rstd", [P, NT])
        th = [sb(f"th{i}", [P, 2, S], F32R) for i in range(2)]
        pr = [sb(f"pr{i}", [P, NT, S]) for i in range(2)]
        pn = [sb(f"pn{i}", [P, NT, S]) for i in range(3)]
        pt = [sb(f"pt{i}", [P, NT * S]) for i in range(2)]
        negmax = sb("negmax", [P, 4, NT])
        raw_negmax = sb("raw_negmax", [P, 4, NT])
        den = sb("den", [P, 4, NT])
        rden = sb("rden", [P, 4, NT])

        ps_t = ctx.enter_context(nc.psum_tensor("ps_t", [P, 512], F32))
        ps_s = [ctx.enter_context(nc.psum_tensor(f"ps_s{i}", [P, NT, S], F32)) for i in range(2)]
        ps_p = ctx.enter_context(nc.psum_tensor("ps_p", [P, NT * S], F32))
        ps_o = [ctx.enter_context(nc.psum_tensor(f"ps_o{i}", [P, 512], F32)) for i in range(2)]
        ps_x = [ctx.enter_context(nc.psum_tensor(f"ps_x{i}", [P, 512], F32)) for i in range(2)]

        g_dram = nc.dram_tensor("g_scratch", [4, P, 2, HEADS, P], F32, kind="Internal").ap()
        wv_dram = nc.dram_tensor("wv_scratch", [4, P, 2, INNER], F32, kind="Internal").ap()

        CONST_OPS = 5
        SETUP_CONSTS = 6
        RESIDENT = LAYERS + len(SMALLS)
        x_taken = sem("x_taken")

        const_in = sem("const_in")
        resident_in = sem("resident_in")
        raw_in = [sem(f"raw_in{i}") for i in range(10)]
        raw_used = sem("raw_used")
        g_made = sem("g_made")
        g_hi = sem("g_hi")
        g_lo = sem("g_lo")
        const_done = sem("const_done")
        split_hi = sem("split_hi")
        g_out = [sem(f"g_out{i}") for i in range(4)]
        wv_out = [sem(f"wv_out{i}") for i in range(4)]
        xin = [sem(f"xin{s}") for s in range(SLOTS)]
        g_in = [sem(f"g_in{i}") for i in range(2)]
        wv_in = sem("wv_in")
        wo_in = sem("wo_in")
        out_done = sem("out_done")
        heads = list(range(HEAD_N))
        t_ready = Tally(sem("t_ready"), BIG_HEADS)
        s_ready = Tally(sem("s_ready"), heads)
        tr_ready = Tally(sem("tr_ready"), heads)
        o_ready = Tally(sem("o_ready"), heads)
        aux_ready = Tally(sem("aux_ready"), [q["id"] for q in AUX])
        thi_ready = Tally(sem("thi_ready"), BIG_HEADS)
        exp_ready = Tally(sem("exp_ready"), heads)
        o_kept = Tally(sem("o_kept"), GROUPS)
        act_side = Tally(sem("act_side"), [(q["id"], k) for q in ORDER for k in act_parts(q)])
        tlo_ready = Tally(sem("tlo_ready"), BIG_HEADS)
        raw_max = Tally(sem("raw_max"), [n for n in heads if PHASES[head(n)[0]][0] == 1])
        max_ready = Tally(sem("max_ready"), heads)
        rden_ready = Tally(sem("rden_ready"), heads)
        pt_ready = Tally(sem("pt_ready"), heads)
        dve_side = Tally(sem("dve_side"), [(q["id"], k) for q in ORDER for k in dve_parts(q)])
        pn_ready = Tally(sem("pn_ready"), heads)
        rstd_ready = Tally(sem("rstd_ready"),
                           [q["id"] for q in ORDER if "ve" in dve_parts(q)])

        def col(name):
            return cols[:, COLS[name]:COLS[name] + 1]

        def f32(ap):
            return ap.bitcast(F32)

        areas = [v[0][:, 0:1024], v[0][:, 1024:2048], v[1][:, 0:1024], v[1][:, 1024:2048],
                 ot[:, :, :].rearrange("p a b -> p (a b)")[:, 0:1024],
                 ot[:, :, :].rearrange("p a b -> p (a b)")[:, 1024:2048],
                 ft[:, :, :].rearrange("p a b -> p (a b)")]
        NA = len(areas)

        def wide(ap):
            return ap.rearrange("p a b -> p (a b)")

        jobs = []
        for i in (2, 3, 0, 1):
            jobs.append(dict(kind="g", i=i, src=[a[f"wqt{i}"], a[f"wkt{i}"]]))
            jobs.append(dict(kind="split", src=[a[f"wv{i}"]], scale=1.0, store=i))
        split_to = {2: (wide(qs[0][:, :, :]), wide(ks[0][:, :, :])),
                    3: (wide(qs[1][:, :, :]), wide(ks[1][:, :, :])),
                    0: (wv_ring[:, 0, :], wv_ring[:, 1, :]),
                    1: (wide(qs[0][:, :, :]), wide(ks[0][:, :, :]))}
        for j in jobs:
            if j["kind"] == "split":
                j["hi"], j["lo"] = split_to[j["store"]]
        for l in range(LAYERS):
            jobs.append(dict(kind="split", src=[a[f"w_up{l}"]], scale=1.0, store=None,
                             hi=w_up[l][:, 0, :], lo=w_up[l][:, 1, :]))
        for p in SMALLS:
            for nm, w, sc in (("wq", wq, SMALL_SCALE), ("wk", wk, 1.0), ("wv", wv, 1.0)):
                jobs.append(dict(kind="split", src=[a[f"{nm}{p}s"]], scale=sc, store=None,
                                 hi=w[p][:, 0, :], lo=w[p][:, 1, :]))
        uses = []
        for j, job in enumerate(jobs):
            job["areas"] = []
            for k, src in enumerate(job["src"]):
                job["areas"].append(len(uses))
                uses.append((j, k))
        banks_of = {}
        splits = []
        for j, job in enumerate(jobs):
            if job["kind"] == "g":
                banks_of[j] = [4 * len(banks_of) + k for k in range(4)]
            else:
                job["n"] = len(splits)
                splits.append(j)
        stores = [j for j, job in enumerate(jobs) if job["kind"] == "g" or job["store"] is not None]
        late_stores = [j for j in stores
                       if jobs[j].get("i") in (0, 1) or jobs[j].get("store") == 0]
        stores = [j for j in stores if j not in late_stores]
        setup_banks = [ps_s[0], ps_s[1], ps_o[0], ps_o[1]]

        def raw(u, r, n):
            return areas[u % NA][0:r, 0:n]

        block = ctx.enter_context(nc.Block())

        @block.sync
        def _(sp):
            sp.dma_start(ident[:, :], a["ident"]).then_inc(const_in, 16)
            sp.dma_start(ones[:, :], a["ones"]).then_inc(const_in, 16)
            sp.dma_start(cols[:, :], a["cols"]).then_inc(const_in, 16)
            sp.dma_start(rows[:, :, :], a["rows"]).then_inc(const_in, 16)
            sp.dma_start(xn[:, :, :], a["masks"]).then_inc(const_in, 16)
            sp.dma_start(wide(pr[0][:, :, :]), a["bias_ones"]).then_inc(const_in, 16)
            for s in range(SLOTS):
                sp.dma_start(x_in[s][:, :, :], a["x"][s]).then_inc(xin[s], 16)
                sp.dma_start(c_in[s][:, :], a["c"][s]).then_inc(xin[s], 16)
                sp.dma_start(m_in[s][:, :, :], a["m"][s:s + 1]).then_inc(xin[s], 16)

            def free_area(u):
                j = uses[u - NA][0]
                if jobs[j]["kind"] == "g":
                    sp.wait_ge(g_made, banks_of[j][-1] + 1)
                else:
                    sp.wait_ge(raw_used, jobs[j]["n"] + 1)

            def store(j):
                job = jobs[j]
                if job["kind"] == "g":
                    i, r = job["i"], rows_of(BIGS[job["i"]])
                    sp.wait_ge(g_lo, banks_of[j][-1] + 1)
                    sp.dma_start(g_dram[i][:, :, :, 0:r], f32(g_ring[i % 2][:, :, :, 0:r])).then_inc(g_out[i], 16)
                else:
                    i = job["store"]
                    r = rows_of(BIGS[i])
                    sp.wait_ge(raw_used, job["n"] + 1)
                    for k, part in enumerate(("hi", "lo")):
                        sp.dma_start(wv_dram[i][0:r, k, :], f32(job[part])[0:r, :]).then_inc(wv_out[i], 16)

            for u, (j, k) in enumerate(uses):
                if u >= NA:
                    jj = uses[u - NA][0]
                    while stores and stores[0] <= jj:
                        store(stores.pop(0))
                    free_area(u)
                src = jobs[j]["src"][k]
                r, n = src.shape
                sp.dma_start(raw(u, r, n), src).then_inc(raw_in[u % NA], 16)
            while stores:
                store(stores.pop(0))
            sp.dma_start(wo_ring[:, :, :], a["wo0"]).then_inc(wo_in, 16)
            for l in range(LAYERS):
                sp.dma_start(w_down[l][:, :, :], a[f"w_down{l}"]).then_inc(resident_in, 16)
            for p in SMALLS:
                sp.dma_start(wo[p][:, :, :], a[f"wo{p}s"]).then_inc(resident_in, 16)
            for j in late_stores:
                store(j)
            sp.sem_inc(g_in[0], 16)
            sp.sem_inc(g_in[1], 16)
            sp.sem_inc(wv_in, 16)
            sp.sem_inc(out_done, 16)

            with sp.Fori(0, TURNS) as turn:

                def load_inputs(r):
                    for s in range(SLOTS):
                        sp.wait_ge(x_taken, (turn * ROUNDS + r) * SLOTS + s + 1)
                        b = (turn * ROUNDS + r + 1) * SLOTS + s
                        sp.dma_start(x_in[s][:, :, :], a["x"][bass.ds(b, 1)].rearrange("o p t d -> (o p) t d")).then_inc(xin[s], 16)
                        sp.dma_start(c_in[s][:, :], a["c"][bass.ds(b, 1)].rearrange("o p t -> (o p) t")).then_inc(xin[s], 16)
                        sp.dma_start(m_in[s][:, :, :], a["m"][bass.ds(b, 1)]).then_inc(xin[s], 16)

                for r in range(ROUNDS):
                    for i in range(4):
                        nxt = (i + 1) % 4
                        p = r * NP + BIGS[i]
                        sp.wait_ge(*aux_ready.after(find("v", p=p, s=1, j=3)["id"], turn))
                        sp.wait_ge(wv_out[i], 32)
                        sp.wait_ge(wv_out[nxt], 32)
                        w = rows_of(BIGS[nxt])
                        sp.dma_start(f32(wv_ring[0:w, :, :]), wv_dram[nxt][0:w]).then_inc(wv_in, 16)
                        sp.wait_ge(*t_ready.after(first_head(p, 1) + HEADS - 1, turn))
                        gi = (i + 2) % 4
                        sp.wait_ge(g_out[i], 16)
                        sp.wait_ge(g_out[gi], 16)
                        w = rows_of(BIGS[gi])
                        sp.dma_start(f32(g_ring[i % 2][:, :, :, 0:w]), g_dram[gi][:, :, :, 0:w]).then_inc(g_in[i % 2], 16)
                        sp.wait_ge(*aux_ready.after(find("y", p=p, s=1)["id"], turn))
                        sp.dma_start(wo_ring[:, :, :], a[f"wo{nxt}"]).then_inc(wo_in, 16)
                        if i == 0:
                            load_inputs(r)
                    for s in range(SLOTS):
                        sp.wait_ge(*dve_side.after((find("f", p=r * NP + NP - 1, s=s)["id"], "x"), turn))
                        b = (turn * ROUNDS + r) * SLOTS + s
                        sp.dma_start(out[bass.ds(b, 1)].rearrange("o p t d -> (o p) t d"), x3[:, :, :]).then_inc(out_done, 16)
            sp.wait_ge(out_done, 16 * (B + 1))
            for s in range(SLOTS):
                sp.wait_ge(xin[s], 48 * (ROUNDS * TURNS + 1))
            sp.wait_ge(g_in[0], 16 * (2 * ROUNDS * TURNS + 1))
            sp.wait_ge(g_in[1], 16 * (2 * ROUNDS * TURNS + 1))
            sp.wait_ge(wv_in, 16 * (4 * ROUNDS * TURNS + 1))
            sp.wait_ge(wo_in, 16 * (4 * ROUNDS * TURNS + 1))

        @block.tensor
        def _(pe):
            def three(o, w_hi, w_lo, m_hi, m_lo, stop=True):
                pe.matmul(o, w_hi, m_lo, start=True, stop=False)
                pe.matmul(o, w_lo, m_hi, start=False, stop=False)
                return pe.matmul(o, w_hi, m_hi, start=False, stop=stop)

            for j, job in enumerate(jobs):
                if job["kind"] != "g":
                    continue
                r = rows_of(BIGS[job["i"]])
                uq, uk = job["areas"]
                pe.wait_ge(raw_in[uq % NA], 16 * (uq // NA + 1))
                pe.wait_ge(raw_in[uk % NA], 16 * (uk // NA + 1))
                for half in range(2):
                    for par in range(2):
                        n = banks_of[j][2 * half + par]
                        if n >= 4:
                            pe.wait_ge(g_lo, n - 3)
                        for t in range(4):
                            pair = 4 * half + t
                            last = pe.matmul(
                                setup_banks[n % 4][:, :, :].rearrange("p a b -> p (a b)")[:, t * P:t * P + r]
                                if n % 4 < 2 else setup_banks[n % 4][:, t * P:t * P + r],
                                raw(uq, P, 1024)[64 * par:64 * par + 64, pair * P:(pair + 1) * P],
                                raw(uk, P, 8 * r)[64 * par:64 * par + 64, pair * r:(pair + 1) * r],
                                start=True, stop=True)
                        last.then_inc(g_made, 1)
            pe.wait_ge(const_in, 16 * SETUP_CONSTS)
            pe.wait_ge(raw_used, len(splits))
            pe.wait_ge(const_done, CONST_OPS)
            pe.wait_ge(g_lo, 16)

            with pe.Fori(0, TURNS) as turn:

                def source(q):
                    p, s = q["p"], q["s"]
                    if q["kind"] == "q" or PHASES[p][1]:
                        return ht[s], D
                    return ct[s], C

                def source_made(q):
                    p, s = q["p"], q["s"]
                    if q["kind"] == "q" or PHASES[p][1]:
                        return q["h"]["id"], "lo"
                    return find("in", p=p // NP * NP, s=s)["id"], "clo"

                def await_inputs(q):
                    kind = q["kind"]
                    by_dve, by_act = [], []
                    if q["aux"] >= 2:
                        before = AUX[q["aux"] - 2]
                        if dve_parts(before):
                            by_dve.append((before["id"], dve_parts(before)[-1]))
                        else:
                            by_act.append((before["id"], act_parts(before)[-1]))
                    if kind == "h":
                        by_dve.append((q["x"]["id"], "x" if q["ln"] is None else "xn1"))
                    elif kind == "ff":
                        by_dve.append((q["h"]["id"], "lo"))
                    elif kind == "f":
                        for ff in q["ffs"]:
                            if dve_parts(ff):
                                by_dve.append((ff["id"], "ff"))
                            else:
                                by_act.append((ff["id"], "ff1"))
                    else:
                        by_dve.append(source_made(q))
                    if by_dve:
                        pe.wait_ge(*dve_side.after(dve_side.last(by_dve), turn))
                    if by_act:
                        pe.wait_ge(*act_side.after(act_side.last(by_act), turn))

                def bias_row(o, name, stop=True):
                    i = ROWS[name]
                    r = 32 * (i % 4)
                    return pe.matmul(o, ones[r:r + 1, :], rows[r:r + 1, i // 4, :], start=False, stop=stop)

                def out_projection(q, part):
                    p, s = q["p"], q["s"]
                    groups = [g for g in GROUPS if g[:2] == (p, s)]
                    start, end = (len(groups) * k // Y_PARTS for k in (part, part + 1))
                    if part == 0:
                        before = AUX[q["aux"] - 2]
                        if dve_parts(before):
                            pe.wait_ge(*dve_side.after((before["id"], dve_parts(before)[-1]), turn))
                        else:
                            pe.wait_ge(*act_side.after((before["id"], act_parts(before)[-1]), turn))
                        if not PHASES[p][2]:
                            pe.wait_ge(resident_in, 16 * RESIDENT)
                        else:
                            pe.wait_ge(wo_in, turn * 64 * ROUNDS + 16 * (big_number(p) + 1))
                    pe.wait_ge(*o_kept.after(groups[end - 1], turn))
                    w = wo_ring if PHASES[p][2] else wo[p % NP]
                    for t in range(NT):
                        o = ps_x[q["aux"] % 2][:, t * D:(t + 1) * D]
                        for g in range(start, end):
                            last = pe.matmul(o, ot[:, g, t * P:(t + 1) * P], w[:, g, :],
                                             start=(g == 0 and t == 0), stop=False)
                        if part == Y_PARTS - 1:
                            last = bias_row(o, f"yo{p % NP}", stop=(t == NT - 1))
                    return last

                def piece(q):
                    kind, s = q["kind"], q["s"]
                    if kind not in AUX_KINDS:
                        return
                    if kind != "y":
                        await_inputs(q)
                    bank = ps_x[q["aux"] % 2]
                    if kind == "y":
                        last = out_projection(q, Y_PARTS - 1)
                    elif kind == "h":
                        src = x[s] if q["ln"] is None else xn
                        for t in range(NT):
                            last = pe.transpose(bank[:, t * P:(t + 1) * P], src[:, t, :], ident[:, :])
                    elif kind == "ff":
                        l, j = q["layer"], q["j"]
                        blocks = (j, j + 4) if l in (0, 2) else (2 * j, 2 * j + 1)
                        for k, c in enumerate(blocks):
                            last = three(bank[:, k * S:(k + 1) * S], w_up[l][:, 0, c * P:(c + 1) * P],
                                         w_up[l][:, 1, c * P:(c + 1) * P], ht[s][:, 0, :], ht[s][:, 1, :])
                    elif kind == "f":
                        l = q["layer"]
                        pe.wait_ge(resident_in, 16 * RESIDENT)
                        for t in range(NT):
                            o = bank[:, t * D:(t + 1) * D]
                            for j in range(FF // P):
                                pe.matmul(o, ft[:, j, t * P:(t + 1) * P], w_down[l][:, j, :], start=(j == 0), stop=False)
                            last = bias_row(o, f"fo{l}")
                    elif kind in ("q", "k"):
                        src, r = source(q)
                        p, j = q["p"], q["j"]
                        w = (wq if kind == "q" else wk)[p % NP]
                        for k in range(2):
                            g = 2 * j + k
                            o = bank[:, k * S:(k + 1) * S]
                            masked = kind == "k" and PHASES[p][0] == 1
                            last = three(o, w[0:r, 0, g * P:(g + 1) * P], w[0:r, 1, g * P:(g + 1) * P],
                                         src[0:r, 0, :], src[0:r, 1, :], stop=not masked)
                            if masked:
                                last = pe.matmul(o, mask_rows[:, :], mask[s][:, p % NP - 2, :], start=False, stop=True)
                    elif kind == "v":
                        src, r = source(q)
                        p, j = q["p"], q["j"]
                        if PHASES[p][2]:
                            pe.wait_ge(wv_in, turn * 64 * ROUNDS + 16 * (big_number(p) + 1))
                            t, half = j // 2, j % 2
                            w_hi = wv_ring[0:r, 0, half * 512:(half + 1) * 512]
                            w_lo = wv_ring[0:r, 1, half * 512:(half + 1) * 512]
                        else:
                            t = j
                            w_hi, w_lo = wv[p % NP][0:r, 0, :], wv[p % NP][0:r, 1, :]
                        last = three(bank[:, :], src[0:r, 0, t * P:(t + 1) * P], src[0:r, 1, t * P:(t + 1) * P],
                                     w_hi, w_lo, stop=PHASES[p][2])
                        if not PHASES[p][2]:
                            o = bank[:, :].rearrange("p (h e) -> p h e", e=32)[:, :, 0:DS]
                            i = ROWS[f"vb{p % NP}"]
                            rr = 32 * (i % 4)
                            last = pe.matmul(o, ones[rr:rr + 1, :], rows[rr:rr + 1, i // 4, :].rearrange("p (h e) -> p h e", e=DS),
                                             start=False, stop=True)
                    last.then_inc(aux_ready.sem, 1)

                def make_t(n):
                    p, s, h = head(n)
                    if not PHASES[p][2]:
                        return
                    i = big_number(p)
                    if h == 0:
                        pe.wait_ge(*dve_side.after((find("v", p=p, s=s, j=0)["h"]["id"], "lo"), turn))
                        if s == 0:
                            pe.wait_ge(g_in[i % 2], turn * 32 * ROUNDS + 16 * (i // 2 + 1))
                    if n - 1 in tlo_ready.at:
                        pe.wait_ge(*tlo_ready.after(n - 1, turn))
                    elif BIG_HEADS.index(n) > 0:
                        pe.wait_ge(*tlo_ready.after(BIG_HEADS[BIG_HEADS.index(n) - 1], turn))
                    r = rows_of(p)
                    g = g_ring[i % 2]
                    three(ps_t[0:r, 0:S], g[:, 0, h, 0:r], g[:, 1, h, 0:r], ht[s][:, 0, :],
                          ht[s][:, 1, :]).then_inc(t_ready.sem, 1)

                def scores(n):
                    p, s, h = head(n)
                    bank = ps_s[n % 2]
                    if n >= 2:
                        pe.wait_ge(*exp_ready.after(n - 2, turn))
                    causal_phase = PHASES[p][0] == 1 and PHASES[p][1]
                    if PHASES[p][2]:
                        pe.wait_ge(*tlo_ready.after(n, turn))
                        if h == 0 and not PHASES[p][1]:
                            pe.wait_ge(*dve_side.after((find("in", p=p // NP * NP, s=s)["id"], "clo"), turn))
                        r = rows_of(p)
                        src = ht[s] if PHASES[p][1] else ct[s]
                        for t in range(NT):
                            last = three(bank[:, t, :], th[n % 2][0:r, 0, t * P:(t + 1) * P],
                                         th[n % 2][0:r, 1, t * P:(t + 1) * P], src[0:r, 0, :], src[0:r, 1, :])
                    else:
                        if h % 8 == 0:
                            pe.wait_ge(*dve_side.after((find("k", p=p, s=s, j=h // 8)["id"], "1"), turn))
                        g, r = h // 4, 32 * (h % 4)
                        for t in range(NT):
                            w = P * (t + 1) if causal_phase else S
                            last = pe.matmul(bank[:, t, 0:w], qs[s][r:r + 32, g, t * P:(t + 1) * P],
                                             ks[s][r:r + 32, g, 0:w], start=True, stop=not causal_phase)
                            if causal_phase:
                                last = pe.matmul(bank[:, t, t * P:(t + 1) * P], ident_bf[:, :], causal[:, :],
                                                 start=False, stop=True)
                    last.then_inc(s_ready.sem, 1)

                def turn_p(n):
                    p, s, h = head(n)
                    pe.wait_ge(*pn_ready.after(n, turn))
                    if n >= 1:
                        pe.wait_ge(*pt_ready.after(n - 1, turn))
                    causal_phase = PHASES[p][0] == 1 and PHASES[p][1]
                    if causal_phase:
                        blocks = [(0, 0, 0), (0, 1, P), (1, 1, 2 * P)]
                    else:
                        blocks = [(k, t, k * S + t * P) for k in range(NT) for t in range(NT)]
                    for k, t, at in blocks:
                        last = pe.transpose(ps_p[:, at:at + P], pn[n % 3][:, t, k * P:(k + 1) * P], ident[:, :])
                    last.then_inc(tr_ready.sem, 1)

                def output(n):
                    p, s, h = head(n)
                    g = GROUPS.index(group_of(n))
                    pe.wait_ge(*pt_ready.after(n, turn))
                    if h == 0:
                        q = find("v", p=p, s=s, j=3 if PHASES[p][2] else 1)
                        pe.wait_ge(*act_side.after((q["id"], "v"), turn))
                    if g >= 2 and (n == 0 or group_of(n - 1) != group_of(n)):
                        pe.wait_ge(*o_kept.after(GROUPS[g - 2], turn))
                    bank = ps_o[g % 2]
                    causal_phase = PHASES[p][0] == 1 and PHASES[p][1]
                    for k in range(NT):
                        if PHASES[p][2]:
                            r, m = 64 * (h % 2), 64
                            w = v[s][:, k * INNER + h * DH:k * INNER + (h + 1) * DH]
                        else:
                            r, m = 32 * (h % 4), 32
                            w = v[s][:, k * 512 + h * 32:k * 512 + (h + 1) * 32]
                        if causal_phase and k == 1:
                            o, mov = bank[r:r + m, P:S], pt[n % 2][:, 2 * P:3 * P]
                        else:
                            o, mov = bank[r:r + m, 0:S], pt[n % 2][:, k * S:(k + 1) * S]
                        last = pe.matmul(o, w, mov, start=(k == 0), stop=(k == NT - 1))
                    last.then_inc(o_ready.sem, 1)

                for i in range(FIRST_STEP, LAST_STEP + 1):
                    if 0 <= i - 5 < HEAD_N:
                        turn_p(i - 5)
                    if 0 <= i - 1 < HEAD_N:
                        scores(i - 1)
                    if 0 <= i + 1 < HEAD_N:
                        make_t(i + 1)
                    if 0 <= i - 6 < HEAD_N:
                        output(i - 6)
                    for q in STEPS.get(i, []):
                        piece(q)
                    for ahead in range(1, Y_PARTS):
                        for q in STEPS.get(i + ahead, []):
                            if q["kind"] == "y":
                                out_projection(q, Y_PARTS - 1 - ahead)

        @block.scalar
        def _(act):
            for j, job in enumerate(jobs):
                if job["kind"] == "g":
                    r = rows_of(BIGS[job["i"]])
                    ring = g_ring[job["i"] % 2]
                    if job["i"] < 2:
                        act.wait_ge(g_out[job["i"] + 2], 16)
                    for k in range(4):
                        n = banks_of[j][k]
                        half, par = k // 2, k % 2
                        act.wait_ge(g_made, n + 1)
                        src = (setup_banks[n % 4][:, :, :].rearrange("p a b -> p (a b)") if n % 4 < 2
                               else setup_banks[n % 4][:, :]).rearrange("p (t c) -> p t c", c=P)[:, :, 0:r]
                        dst = ring[:, 0, 8 * half + par:8 * half + par + 7:2, 0:r]
                        act.activation(dst, src, ACT.Copy, scale=BIG_SCALE).then_inc(g_hi, 1)
                else:
                    u = job["areas"][0]
                    r, n = job["src"][0].shape
                    act.wait_ge(raw_in[u % NA], 16 * (u // NA + 1))
                    if job["store"] == 1:
                        act.wait_ge(wv_out[2], 32)
                    act.activation(job["hi"][0:r, :], raw(u, r, n), ACT.Copy, scale=job["scale"]).then_inc(split_hi, 1)

            with act.Fori(0, TURNS) as turn:

                def piece(q):
                    kind, s = q["kind"], q["s"]
                    if kind == "in":
                        act.wait_ge(xin[s], turn * 48 * ROUNDS + 48 * (q["p"] // NP + 1))
                        act.activation(ct[s][:, 0, :], c_in[s][:, :], ACT.Copy).then_inc(act_side.sem, 1)
                    if kind not in AUX_KINDS or not act_parts(q):
                        return
                    act.wait_ge(*aux_ready.after(q["id"], turn))
                    bank, tmp = ps_x[q["aux"] % 2], side[q["aux"] % 2]
                    if kind == "h":
                        if q["ln"] is None:
                            act.activation(tmp[:, 0:S], bank[:, 0:S], ACT.Copy).then_inc(act_side.sem, 1)
                        else:
                            act.activation(tmp[:, 0:S], bank[:, 0:S], ACT.Identity, bias=col(f"b{q['ln']}"),
                                           scale=col(f"g{q['ln']}")).then_inc(act_side.sem, 1)
                    elif kind == "ff":
                        l, j = q["layer"], q["j"]
                        if l in (0, 2):
                            act.activation(tmp[:, 0:S], bank[:, S:2 * S], ACT.Gelu,
                                           bias=col(f"ffb{l}_{4 + j}")).then_inc(act_side.sem, 1)
                        else:
                            for k in range(2):
                                act.activation(ft[:, 2 * j + k, :], bank[:, k * S:(k + 1) * S], ACT.Gelu,
                                               bias=col(f"ffb{l}_{2 * j + k}")).then_inc(act_side.sem, 1)
                    elif kind in ("q", "k"):
                        for k in range(2):
                            name = f"{kind}mb{q['p'] % NP}_{2 * q['j'] + k}"
                            act.activation(tmp[:, k * S:(k + 1) * S].bitcast(F32R), bank[:, k * S:(k + 1) * S],
                                           ACT.Identity, bias=col(name), scale=col("m" + kind)).then_inc(act_side.sem, 1)
                    elif kind == "v":
                        p, j = q["p"], q["j"]
                        act.activation(v[s][:, j * 512:(j + 1) * 512], bank[:, :], ACT.Copy).then_inc(act_side.sem, 1)

                def exps(n):
                    p, s, h = head(n)
                    act.wait_ge(*max_ready.after(n, turn))
                    if n >= 2:
                        act.wait_ge(*pn_ready.after(n - 2, turn))
                    causal_phase = PHASES[p][0] == 1 and PHASES[p][1]
                    for t in range(NT):
                        w = P * (t + 1) if causal_phase else S
                        last = act.activation(pr[n % 2][:, t, 0:w], ps_s[n % 2][:, t, 0:w], ACT.Exp,
                                              bias=negmax[:, n % 4, t:t + 1], accum_out=den[:, n % 4, t:t + 1])
                    last.then_inc(exp_ready.sem, 1)

                def t_high(n):
                    p = head(n)[0]
                    if not PHASES[p][2]:
                        return
                    r = rows_of(p)
                    act.wait_ge(*t_ready.after(n, turn))
                    act.activation(th[n % 2][0:r, 0, :], ps_t[0:r, 0:S], ACT.Copy).then_inc(thi_ready.sem, 1)

                def keep_output(n):
                    if GROUP_LAST[group_of(n)] != n:
                        return
                    act.wait_ge(*o_ready.after(n, turn))
                    g = group_of(n)
                    act.activation(ot[:, g[2], :], ps_o[GROUPS.index(g) % 2][:, 0:S], ACT.Copy).then_inc(o_kept.sem, 1)

                for i in range(FIRST_STEP, LAST_STEP + 1):
                    if 0 <= i < HEAD_N:
                        t_high(i)
                    for q in STEPS.get(i - 1, []):
                        piece(q)
                    if 0 <= i - 7 < HEAD_N:
                        keep_output(i - 7)
                    if 0 <= i - 2 < HEAD_N:
                        exps(i - 2)

        @block.vector
        def _(dve):
            count = [0]

            def const(ins):
                count[0] += 1
                ins.then_inc(const_done, 1)

            dve.wait_ge(const_in, 16 * SETUP_CONSTS)
            const(dve.tensor_copy(ident_bf[:, :], ident[:, :]))
            const(dve.tensor_copy(causal[:, :], xn[:, 0, :]))
            const(dve.tensor_copy(mask_rows[:, :], xn[0:1, 1, :]))
            q0, q1 = COLS[f"qb{SMALLS[0]}_0"], COLS["mq"]
            tmp = side[0][:, 0:q1 - q0]
            const(dve.tensor_tensor(tmp, cols[:, q0:q1], pr[0][:, 0, 0:q1 - q0], ALU.mult))
            dve.wait_ge(const_done, 4)
            const(dve.tensor_tensor(cols[:, q0:q1], tmp, pr[0][:, 1, 0:q1 - q0], ALU.add))
            assert count[0] == CONST_OPS
            for j, job in enumerate(jobs):
                if job["kind"] == "g":
                    r = rows_of(BIGS[job["i"]])
                    ring = g_ring[job["i"] % 2]
                    for k in range(4):
                        n = banks_of[j][k]
                        half, par = k // 2, k % 2
                        dve.wait_ge(g_hi, n + 1)
                        src = (setup_banks[n % 4][:, :, :].rearrange("p a b -> p (a b)") if n % 4 < 2
                               else setup_banks[n % 4][:, :]).rearrange("p (t c) -> p t c", c=P)[:, :, 0:r]
                        h0 = 8 * half + par
                        dve.scalar_tensor_tensor(out=ring[:, 1, h0:h0 + 7:2, 0:r], in0=src, scalar=BIG_SCALE,
                                                 in1=f32(ring[:, 0, h0:h0 + 7:2, 0:r]), op0=ALU.mult,
                                                 op1=ALU.subtract).then_inc(g_lo, 1)
                else:
                    u = job["areas"][0]
                    r, n = job["src"][0].shape
                    dve.wait_ge(split_hi, job["n"] + 1)
                    dve.scalar_tensor_tensor(out=job["lo"][0:r, :], in0=raw(u, r, n), scalar=job["scale"],
                                             in1=f32(job["hi"][0:r, :]), op0=ALU.mult,
                                             op1=ALU.subtract).then_inc(raw_used, 1)

            with dve.Fori(0, TURNS) as turn:

                def tick(ins):
                    ins.then_inc(dve_side.sem, 1)

                def norm_stats(q, part):
                    src = x3 if q["kind"] == "y" and third_sum(q) else x[q["s"]]
                    if part == 1:
                        before = "mask" if q["kind"] == "in" else "x"
                        dve.wait_ge(*dve_side.after((q["id"], before), turn))
                        for t in range(NT):
                            tick(dve.bn_stats(stats[:, t, :], src[:, t, :]))
                    elif part == 2:
                        dve.wait_ge(*dve_side.after((q["id"], "st1"), turn))
                        dve.memset(fence[:, :], 0.0)
                        for t in range(NT):
                            tick(dve.bn_aggr(mv[:, t, :], stats[:, t, :]))
                        dve.wait_ge(*dve_side.after((q["id"], "mv1"), turn))
                        tick(dve.tensor_scalar(ve[:, :], mv[:, :, 1], EPS, None, ALU.add))
                        if q["kind"] == "in":
                            dve.wait_ge(*dve_side.after((q["id"], "ve"), turn))
                            dve.sem_inc(x_taken, 1)

                def piece(q, part):
                    kind, s = q["kind"], q["s"]
                    if kind == "xn" and part == 1:
                        before = [o for o in ORDER[:ORDER.index(q)] if o["s"] == s and "ve" in dve_parts(o)][-1]
                        dve.wait_ge(*rstd_ready.after(before["id"], turn))
                        src = x3 if third_sum(q) else x[s]
                        for t in range(NT):
                            tick(dve.tensor_scalar(xn[:, t, :], src[:, t, :], mv[:, t, 0:1], rstd[:, t:t + 1],
                                                   ALU.subtract, ALU.mult))
                        if third_sum(q):
                            tick(dve.tensor_tensor(x[s][:, :, :], x[s][:, :, :], x3[:, :, :], ALU.add))
                    if part > 0:
                        if "ve" in dve_parts(q):
                            norm_stats(q, part)
                        elif kind == "h" and part == 1:
                            dve.wait_ge(*dve_side.after((q["id"], "hi"), turn))
                            tick(dve.tensor_tensor(ht[s][:, 1, :], side[q["aux"] % 2][:, 0:S], f32(ht[s][:, 0, :]),
                                                   ALU.subtract))
                        return
                    if kind == "in":
                        dve.wait_ge(xin[s], turn * 48 * ROUNDS + 48 * (q["p"] // NP + 1))
                        if q["p"] > 0:
                            dve.wait_ge(*dve_side.after((find("f", p=q["p"] - 1, s=s)["id"], "x"), turn))
                        tick(dve.tensor_copy(x[s][:, :, :], x_in[s][:, :, :]))
                        dve.wait_ge(*act_side.after((q["id"], "chi"), turn))
                        tick(dve.tensor_tensor(ct[s][:, 1, :], c_in[s][:, :], f32(ct[s][:, 0, :]), ALU.subtract))
                        tick(dve.tensor_scalar(mask[s][:, :, :], m_in[s][:, :, :], BIG, None, ALU.mult))
                    elif kind == "y":
                        bank = ps_x[q["aux"] % 2][:, 0:S].rearrange("p (t d) -> p t d", d=D)
                        dve.wait_ge(*aux_ready.after(q["id"], turn))
                        if third_sum(q):
                            b = turn * ROUNDS * SLOTS + q["p"] // NP * SLOTS + s
                            dve.wait_ge(out_done, b * 16 + 16)
                            tick(dve.tensor_copy(x3[:, :, :], bank))
                        else:
                            tick(dve.tensor_tensor(x[s][:, :, :], bank, x[s][:, :, :], ALU.add))
                    elif kind == "f":
                        bank = ps_x[q["aux"] % 2][:, 0:S].rearrange("p (t d) -> p t d", d=D)
                        dve.wait_ge(*aux_ready.after(q["id"], turn))
                        if q["p"] % NP + 1 < NP:
                            tick(dve.tensor_tensor(x[s][:, :, :], bank, x[s][:, :, :], ALU.add))
                        else:
                            tick(dve.tensor_tensor(x3[:, :, :], bank, x[s][:, :, :], ALU.add))
                    elif kind == "h":
                        tmp = side[q["aux"] % 2]
                        dve.wait_ge(*act_side.after((q["id"], "h"), turn))
                        tick(dve.tensor_copy(ht[s][:, 0, :], tmp[:, 0:S]))
                    elif kind == "ff" and dve_parts(q):
                        l, j = q["layer"], q["j"]
                        dve.wait_ge(*act_side.after((q["id"], "ff"), turn))
                        tick(dve.scalar_tensor_tensor(out=ft[:, j, :], in0=ps_x[q["aux"] % 2][:, 0:S],
                                                      scalar=col(f"ffb{l}_{j}"), in1=side[q["aux"] % 2][:, 0:S],
                                                      op0=ALU.add, op1=ALU.mult))
                    elif kind in ("q", "k"):
                        dst = (qs if kind == "q" else ks)[s]
                        dve.wait_ge(*act_side.after((q["id"], "1"), turn))
                        for k in range(2):
                            g = 2 * q["j"] + k
                            tick(dve.scalar_tensor_tensor(out=dst[:, g, :], in0=ps_x[q["aux"] % 2][:, k * S:(k + 1) * S],
                                                          scalar=col(f"{kind}b{q['p'] % NP}_{g}"),
                                                          in1=side[q["aux"] % 2][:, k * S:(k + 1) * S],
                                                          op0=ALU.add, op1=ALU.subtract))

                def t_low(n):
                    p = head(n)[0]
                    if not PHASES[p][2]:
                        return
                    r = rows_of(p)
                    dve.wait_ge(*thi_ready.after(n, turn))
                    dve.tensor_tensor(th[n % 2][0:r, 1, :], ps_t[0:r, 0:S], f32(th[n % 2][0:r, 0, :]),
                                      ALU.subtract).then_inc(tlo_ready.sem, 1)

                def row_max(n):
                    p = head(n)[0]
                    dve.wait_ge(*s_ready.after(n, turn))
                    bank = ps_s[n % 2]
                    if PHASES[p][0] != 1:
                        dve.tensor_reduce(negmax[:, n % 4, :], bank[:, :, :], AX.X, ALU.max,
                                          negate=True).then_inc(max_ready.sem, 1)
                        return
                    if PHASES[p][1]:
                        dve.tensor_reduce(raw_negmax[:, n % 4, 0:1], bank[:, 0, 0:P], AX.X, ALU.max, negate=True)
                        dve.tensor_reduce(raw_negmax[:, n % 4, 1:2], bank[:, 1, :], AX.X, ALU.max,
                                          negate=True).then_inc(raw_max.sem, 1)
                    else:
                        dve.tensor_reduce(raw_negmax[:, n % 4, :], bank[:, :, :], AX.X, ALU.max,
                                          negate=True).then_inc(raw_max.sem, 1)
                    dve.wait_ge(*raw_max.after(n, turn))
                    dve.tensor_scalar(negmax[:, n % 4, :], raw_negmax[:, n % 4, :], 8.0, 0.125, ALU.mult,
                                      ALU.mult).then_inc(max_ready.sem, 1)

                def over_sum(n):
                    dve.wait_ge(*exp_ready.after(n, turn))
                    dve.reciprocal(rden[:, n % 4, :], den[:, n % 4, :]).then_inc(rden_ready.sem, 1)

                def keep_pt(n):
                    p = head(n)[0]
                    dve.wait_ge(*tr_ready.after(n, turn))
                    w = 3 * P if PHASES[p][0] == 1 and PHASES[p][1] else NT * S
                    dve.tensor_copy(pt[n % 2][:, 0:w], ps_p[:, 0:w]).then_inc(pt_ready.sem, 1)

                for i in range(FIRST_STEP, LAST_STEP + 1):
                    if 0 <= i < HEAD_N:
                        t_low(i)
                    if 0 <= i - 3 < HEAD_N:
                        over_sum(i - 3)
                    if 0 <= i - 5 < HEAD_N:
                        keep_pt(i - 5)
                    for q in STEPS.get(i - 1, []):
                        piece(q, 0)
                    if 0 <= i - 1 < HEAD_N:
                        row_max(i - 1)
                    for q in STEPS.get(i - 1, []):
                        piece(q, 1)
                    for q in STEPS.get(i - 1, []):
                        piece(q, 2)

        @block.gpsimd
        def _(pool):
            pool.wait_ge(const_in, 16 * SETUP_CONSTS)
            neghalf = cols[:, COLS["neghalf0"]:COLS["neghalf0"] + NT]
            with pool.Fori(0, TURNS) as turn:

                def normalise(n):
                    p = head(n)[0]
                    pool.wait_ge(*rden_ready.after(n, turn))
                    if n >= 3:
                        pool.wait_ge(*tr_ready.after(n - 3, turn))
                    if PHASES[p][0] == 1 and PHASES[p][1]:
                        for t in range(NT):
                            w = P * (t + 1)
                            last = pool.tensor_tensor(pn[n % 3][:, t, 0:w], pr[n % 2][:, t, 0:w],
                                                      rden[:, n % 4, t:t + 1].to_broadcast([P, w]), ALU.mult)
                    else:
                        last = pool.tensor_tensor(pn[n % 3][:, :, :], pr[n % 2][:, :, :],
                                                  rden[:, n % 4, :].unsqueeze(2).to_broadcast([P, NT, S]), ALU.mult)
                    last.then_inc(pn_ready.sem, 1)

                def piece(q):
                    if "ve" in dve_parts(q):
                        pool.wait_ge(*dve_side.after((q["id"], "ve"), turn))
                        pool.tensor_tensor(rstd[:, :], ve[:, :], neghalf, ALU.pow).then_inc(rstd_ready.sem, 1)

                for i in range(FIRST_STEP, LAST_STEP + 1):
                    if 0 <= i - 3 < HEAD_N:
                        normalise(i - 3)
                    for q in STEPS.get(i - 1, []):
                        piece(q)


def stacked(w, order):
    r = w.shape[0]
    o = np.zeros((r, HEADS, 32), w.dtype)
    for at in order:
        o[:, :, at:at + DS] = w.reshape(r, HEADS, DS)
    return np.ascontiguousarray(o.reshape(r, HEADS * 32))


def layout(i):
    f = {k: np.asarray(w) for k, w in i.items()}
    a = {}
    rows_in = list(range(B)) + list(range(SLOTS))
    a["x"] = np.ascontiguousarray(f["x"].reshape(B, NT, P, D).transpose(0, 2, 1, 3)[rows_in])
    a["c"] = np.ascontiguousarray(f["ctx_768"].transpose(0, 2, 1)[rows_in])
    a["m"] = np.ascontiguousarray(np.stack([f["mask_BxS_bf0"], f["mask_BxS2_bf0"]], 1)[rows_in])
    L0, L1, L2, L3 = (f"L{k}_xattn_" for k in range(4))
    big = [(L0 + "Wq1", L0 + "Wk1", L0 + "Wv1", L0 + "Wo1"), (L0 + "Wq2", L0 + "Wk2", L0 + "Wv2", L0 + "Wo2"),
           (L2 + "a1_wq", L2 + "a1_wk", L2 + "a1_wv", L2 + "a1_wo"),
           (L2 + "a2_wq", L2 + "a2_wk", L2 + "a2_wv", L2 + "a2_wo")]
    for n, (q, k, vv, o) in enumerate(big):
        for nm, w in (("wqt", f[q]), ("wkt", f[k])):
            t = w.T.reshape(HEADS // 2, P, w.shape[0]).transpose(1, 0, 2)
            a[f"{nm}{n}"] = np.ascontiguousarray(t.reshape(P, -1))
        a[f"wv{n}"] = np.ascontiguousarray(f[vv])
        a[f"wo{n}"] = np.ascontiguousarray(f[o].reshape(HEADS // 2, P, D).transpose(1, 0, 2))
    qkv, qkvb = f[L1 + "qkv_w"], f[L1 + "qkv_b"]
    small = {2: (qkv[:, 0:D], qkv[:, D:2 * D], qkv[:, 2 * D:], f[L1 + "proj_w"], qkvb[0:D], qkvb[D:2 * D], qkvb[2 * D:]),
             3: (f[L1 + "q_w"], f[L1 + "k_w"], f[L1 + "v_w"], f[L1 + "out_w"], f[L1 + "q_b"], f[L1 + "k_b"], f[L1 + "v_b"]),
             6: (f[L3 + "Wq"], f[L3 + "Wk"], f[L3 + "Wv"], f[L3 + "Wo"], f[L3 + "bq"], f[L3 + "bk"], f[L3 + "bv"])}
    Q_ALL, K_ALL, Q_LO, K_LO = (0, 8, 16), (0, 8, 16), (16,), (8,)
    cols = np.zeros((P, len(COLS)), np.float32)
    rows = np.zeros((P, ROW_W, D), np.float32)

    def put_row(name, w):
        rows[32 * (ROWS[name] % 4), ROWS[name] // 4, :] = w

    for p, (q, k, vv, o, bq, bk, bv) in small.items():
        a[f"wq{p}s"], a[f"wk{p}s"], a[f"wv{p}s"] = stacked(q, Q_ALL), stacked(k, K_ALL), stacked(vv, (0,))
        oo = np.zeros((QUADS, 4, 32, D), np.float32)
        oo[:, :, 0:DS] = o.reshape(QUADS, 4, DS, D)
        a[f"wo{p}s"] = np.ascontiguousarray(oo.reshape(QUADS, P, D).transpose(1, 0, 2))
        for kind, w, places in (("qb", bq, Q_ALL), ("qmb", bq, Q_LO), ("kb", bk, K_ALL), ("kmb", bk, K_LO)):
            t = stacked(w.reshape(1, -1), places).reshape(QUADS, P)
            for g in range(QUADS):
                cols[:, COLS[f"{kind}{p}_{g}"]] = t[g]
        put_row(f"vb{p}", bv)
    lns = [L0 + "g1", L0 + "g2", L0 + "g3", L1 + "ln1_w", L1 + "ln2_w", L1 + "ln3_w",
           L2 + "ln1_g", L2 + "ln2_g", L2 + "ln3_g", L3 + "ln_g"]
    lnb = [L0 + "b1", L0 + "b2", L0 + "b3", L1 + "ln1_b", L1 + "ln2_b", L1 + "ln3_b",
           L2 + "ln1_b", L2 + "ln2_b", L2 + "ln3_b", L3 + "ln_b"]
    for n in range(10):
        cols[:, COLS[f"g{n}"]] = f[lns[n]]
        cols[:, COLS[f"b{n}"]] = f[lnb[n]]
    ff = [(L0 + "Wp", L0 + "bp", L0 + "Wf", L0 + "bf"), (L1 + "mlp1_w", L1 + "mlp1_b", L1 + "mlp2_w", L1 + "mlp2_b"),
          (L2 + "ff_w1", L2 + "ff_b1", L2 + "ff_w2", L2 + "ff_b2"), (L3 + "W1", L3 + "b1", L3 + "W2", L3 + "b2")]
    for l, (w1, b1, w2, b2) in enumerate(ff):
        a[f"w_up{l}"] = np.ascontiguousarray(f[w1])
        a[f"w_down{l}"] = np.ascontiguousarray(f[w2].reshape(FF // P, P, D).transpose(1, 0, 2))
        for j in range(f[b1].shape[0] // P):
            cols[:, COLS[f"ffb{l}_{j}"]] = f[b1][j * P:(j + 1) * P]
        put_row(f"fo{l}", f[b2])
    outs = [L0 + "bo1", L0 + "bo2", L1 + "proj_b", L1 + "out_b", L2 + "a1_bo", L2 + "a2_bo", L3 + "bo"]
    for p, nm in enumerate(outs):
        put_row(f"yo{p}", f[nm])
    r32 = np.arange(P) % 32
    cols[:, COLS["mq"]] = (r32 >= 16) & (r32 < 24)
    cols[:, COLS["mk"]] = (r32 >= 8) & (r32 < 16)
    cols[:, COLS["neghalf0"]] = cols[:, COLS["neghalf1"]] = -0.5
    a["cols"], a["rows"] = cols, rows
    a["ident"], a["ones"] = np.eye(P, dtype=np.float32), np.ones((P, P), np.float32)
    masks = np.zeros((P, NT, D), np.float32)
    masks[:, 0, :] = np.where(np.arange(P)[None, :] > np.arange(P)[:, None], np.float32(BIG), np.float32(0))
    masks[0, 1, :] = r32 == 24
    a["masks"] = masks
    fix = np.zeros((P, NT, S), np.float32)
    q0, q1 = COLS[f"qb{SMALLS[0]}_0"], COLS["mq"]
    for name, c in COLS.items():
        if q0 <= c < q1:
            fix[:, 0, c - q0] = np.float32(SMALL_SCALE) if name[0] == "q" else 1.0
            if name.startswith(("qb2", "qb3")):
                fix[:, 1, c - q0] = r32 == 24
    a["bias_ones"] = np.ascontiguousarray(fix.reshape(P, NT * S))
    return a


def kernel(**inputs):
    import concourse.bacc as bacc
    from concourse.bass_utils import run_bass_kernel_spmd

    arrays = {f"in_{k}": w for k, w in layout(inputs).items()}
    nc = bacc.Bacc("TRN2", target_bir_lowering=False, num_devices=1)
    aps = {k[3:]: nc.dram_tensor(k, w.shape, mybir.dt.from_np(w.dtype), kind="ExternalInput").ap()
           for k, w in arrays.items()}
    out = nc.dram_tensor("out_0", (B, P, NT, D), F32, kind="ExternalOutput").ap()
    build(nc, aps, out)
    r = run_bass_kernel_spmd(nc, [arrays], core_ids=[0])
    y = r.results[0]["out_0"]
    return np.ascontiguousarray(y.transpose(0, 2, 1, 3)).reshape(B, S, D)
```
